# Optimizing a Trainium2 kernel written in Bass

```python
import numpy as np
import jax
import jax.numpy as jnp

def _softmax(x, axis=-1):
    return jax.nn.softmax(x, axis=axis)

def _gelu(x):
    return jax.nn.gelu(x, approximate=True)

def _silu(x):
    return jax.nn.silu(x)

def _sigmoid(x):
    return jax.nn.sigmoid(x)

def _layernorm(x, axis=-1, eps=1e-05):
    m = jnp.mean(x, axis=axis, keepdims=True)
    v = jnp.var(x, axis=axis, keepdims=True)
    return (x - m) / jnp.sqrt(v + eps)

def _scatter_add(tgt, idx, src, axis=0):
    return tgt.at[idx].add(src)

def _segment_sum(src, seg, n):
    return jax.ops.segment_sum(src, seg, n)
kernel_name = 'mk_seq_postln_d1_jaxref_r8_e421c1'

def setup_inputs(seed: int=0):
    np.random.seed(seed)
    _w = jnp.asarray

    def _L0_attn_setup():
        import jax, jax.numpy as jnp
        import numpy as np
        NEG_INF = -1e+30

        def rotary_pos_emb(x):
            B, T, H, D = x.shape
            exponents = (jnp.arange(0, D, 2)[:D // 2] // D).astype(jnp.float32)
            freqs = 1.0 / jnp.power(jnp.float32(1000.0), exponents)
            theta = jnp.arange(T, dtype=jnp.float32)[:, None] * freqs[None, :]
            cos = jnp.cos(theta)[None, :, None, :]
            sin = jnp.sin(theta)[None, :, None, :]
            xr = x.astype(jnp.float32).reshape(B, T, H, D // 2, 2)
            x0, x1 = (xr[..., 0], xr[..., 1])
            out = jnp.stack([x0 * cos - x1 * sin, x0 * sin + x1 * cos], axis=-1)
            return out.reshape(B, T, H, D).astype(x.dtype)

        def attention_fwd(x, wq, wk, wv, wo, n_heads=32):
            B, T, C = x.shape
            hd = C // n_heads
            xq = (x @ wq.T).reshape(B, T, n_heads, hd)
            xk = (x @ wk.T).reshape(B, T, n_heads, hd)
            xv = (x @ wv.T).reshape(B, T, n_heads, hd)
            xq = rotary_pos_emb(xq)
            xk = rotary_pos_emb(xk)
            scale = hd ** (-0.5)
            scores = jnp.einsum('bqhd,bkhd->bhqk', xq, xk) * scale
            causal = jnp.tril(jnp.ones((T, T), dtype=bool))
            scores = jnp.where(causal[None, None], scores, NEG_INF)
            probs = jax.nn.softmax(scores.astype(jnp.float32), axis=-1).astype(xq.dtype)
            out = jnp.einsum('bhqk,bkhd->bqhd', probs, xv).reshape(B, T, C)
            return out @ wo.T
        key = jax.random.key(seed)
        ks = jax.random.split(key, 5)
        B, T, C = (2, 256, 512)
        s = 0.02
        return {'x': jax.random.normal(ks[0], (B, T, C), jnp.float32), 'wq': jax.random.normal(ks[1], (C, C), jnp.float32) * s, 'wk': jax.random.normal(ks[2], (C, C), jnp.float32) * s, 'wv': jax.random.normal(ks[3], (C, C), jnp.float32) * s, 'wo': jax.random.normal(ks[4], (C, C), jnp.float32) * s}
    _L0_attn_in = _L0_attn_setup()

    def _L0_ffn_setup():
        import jax, jax.numpy as jnp
        import numpy as np
        HIDDEN = 512
        INTER = 1376

        def _ternary_quantize(w):
            scale = jnp.mean(jnp.abs(w))
            return jnp.clip(jnp.round(w / scale), -1.0, 1.0) * scale
        key = jax.random.key(seed)
        kx, kg, ku, kd = jax.random.split(key, 4)
        x = jax.random.normal(kx, (2, 256, HIDDEN), dtype=jnp.float32)
        w_gate = _ternary_quantize(jax.random.normal(kg, (INTER, HIDDEN), dtype=jnp.float32) * 0.02)
        w_up = _ternary_quantize(jax.random.normal(ku, (INTER, HIDDEN), dtype=jnp.float32) * 0.02)
        w_down = _ternary_quantize(jax.random.normal(kd, (HIDDEN, INTER), dtype=jnp.float32) * 0.02)
        return {'x': x, 'w_gate': w_gate, 'w_up': w_up, 'w_down': w_down}
    _L0_ffn_in = _L0_ffn_setup()
    _d = {'L0_attn_x': _L0_attn_in['x'], 'L0_attn_wq': _L0_attn_in['wq'], 'L0_attn_wk': _L0_attn_in['wk'], 'L0_attn_wv': _L0_attn_in['wv'], 'L0_attn_wo': _L0_attn_in['wo'], 'L0_ffn_w_gate': _L0_ffn_in['w_gate'], 'L0_ffn_w_up': _L0_ffn_in['w_up'], 'L0_ffn_w_down': _L0_ffn_in['w_down']}
    _x0 = _d['L0_attn_x']
    _d['L0_attn_x'] = jax.random.normal(jax.random.fold_in(jax.random.key(seed), 1), (4, 256, 512), dtype=_x0.dtype)
    del _x0
    return _d

def reference(L0_attn_x, L0_attn_wq, L0_attn_wk, L0_attn_wv, L0_attn_wo, L0_ffn_w_gate, L0_ffn_w_up, L0_ffn_w_down):

    def _L0_attn_ref(x, wq, wk, wv, wo):
        import jax, jax.numpy as jnp
        import numpy as np
        NEG_INF = -1e+30

        def rotary_pos_emb(x):
            B, T, H, D = x.shape
            exponents = (jnp.arange(0, D, 2)[:D // 2] // D).astype(jnp.float32)
            freqs = 1.0 / jnp.power(jnp.float32(1000.0), exponents)
            theta = jnp.arange(T, dtype=jnp.float32)[:, None] * freqs[None, :]
            cos = jnp.cos(theta)[None, :, None, :]
            sin = jnp.sin(theta)[None, :, None, :]
            xr = x.astype(jnp.float32).reshape(B, T, H, D // 2, 2)
            x0, x1 = (xr[..., 0], xr[..., 1])
            out = jnp.stack([x0 * cos - x1 * sin, x0 * sin + x1 * cos], axis=-1)
            return out.reshape(B, T, H, D).astype(x.dtype)

        def attention_fwd(x, wq, wk, wv, wo, n_heads=32):
            B, T, C = x.shape
            hd = C // n_heads
            xq = (x @ wq.T).reshape(B, T, n_heads, hd)
            xk = (x @ wk.T).reshape(B, T, n_heads, hd)
            xv = (x @ wv.T).reshape(B, T, n_heads, hd)
            xq = rotary_pos_emb(xq)
            xk = rotary_pos_emb(xk)
            scale = hd ** (-0.5)
            scores = jnp.einsum('bqhd,bkhd->bhqk', xq, xk) * scale
            causal = jnp.tril(jnp.ones((T, T), dtype=bool))
            scores = jnp.where(causal[None, None], scores, NEG_INF)
            probs = jax.nn.softmax(scores.astype(jnp.float32), axis=-1).astype(xq.dtype)
            out = jnp.einsum('bhqk,bkhd->bqhd', probs, xv).reshape(B, T, C)
            return out @ wo.T
        return attention_fwd(x, wq, wk, wv, wo)

    def _L0_ffn_ref(x, w_gate, w_up, w_down):
        import jax, jax.numpy as jnp
        import numpy as np
        HIDDEN = 512
        INTER = 1376

        def _ternary_quantize(w):
            scale = jnp.mean(jnp.abs(w))
            return jnp.clip(jnp.round(w / scale), -1.0, 1.0) * scale
        xf = x.astype(jnp.float32) / 128.0
        gate = jnp.einsum('bsh,ih->bsi', xf, w_gate)
        up = jnp.einsum('bsh,ih->bsi', xf, w_up)
        inter = jax.nn.silu(gate) * up
        inter_q = jnp.trunc(jnp.clip(inter * 128.0, -128.0, 127.0)).astype(jnp.int8)
        down = jnp.einsum('bsi,hi->bsh', inter_q.astype(jnp.float32), w_down)
        out = jnp.trunc(jnp.clip(down * 128.0, -128.0, 127.0)).astype(jnp.int8)
        return out
    x = L0_attn_x
    x = _layernorm(x + _L0_attn_ref(x, L0_attn_wq, L0_attn_wk, L0_attn_wv, L0_attn_wo), axis=-1)
    x = _layernorm(x + _L0_ffn_ref(x, L0_ffn_w_gate, L0_ffn_w_up, L0_ffn_w_down), axis=-1)
    return x

_drawn_inputs = setup_inputs


def setup_inputs(seed=0):
    import zlib

    import numpy as np

    out = dict(_drawn_inputs(seed))
    spreads = {}
    factors = {'L0_attn_wq': 8.0, 'L0_attn_wk': 7.902}
    for name, (base, spread) in spreads.items():
        noise = np.random.default_rng([zlib.crc32(name.encode()), seed]).standard_normal(out[name].shape)
        drawn = base * np.exp(spread * noise) if base else spread * noise
        out[name] = jnp.asarray(drawn.astype(out[name].dtype))
    for name, factor in factors.items():
        out[name] = (out[name] * factor).astype(out[name].dtype)
    return out
```

```python
import concourse.bass as bass
from concourse import mybir
from contextlib import ExitStack

F32 = mybir.dt.float32
F32R = mybir.dt.float32r
ALU = mybir.AluOpType
ACT = mybir.ActivationFunctionType

P = 128
B, T, C, H, D = 4, 256, 512, 32, 16
INTER = 1376
NI = -(-INTER // P)
NT = T // P
NTT = B * NT
NC = C // P
NBLK = H // 2
NG = H // 4
SLOT = 64
KROWS = 3 * D
SW = 3 * P
BIG = 1.0e30
HUGE = 3.0e38
MAGIC = 1.5 * 2.0 ** 23
EPS = 1e-5
HALF = 512
NHALF = B * T // HALF

K_ID = 0
K_MASK = K_ID + P
K_ROT = K_MASK + 2 * P
K_HALF = K_ROT + 4 * NT
NK = K_HALF + 1

R_A, R_S, R_PT, R_QKT, R_SM, R_P, R_PTS = 2, 3, 2, 3, 3, 3, 3
LAG_PT, LAG_AV = 3, 5

A_USES = ["dve"] * 4 + ["act"] * 2 + ["act"] * NG + ["dve"] * NT
V_USE, AV_USE, Y_USE = 4, 6, 6 + NG


def layer(nc, xT, x, wqkvo, wgu, wd, consts, out):
    ctx = ExitStack()
    with ctx:
        def sb(name, shape, dt, where=ctx):
            return where.enter_context(nc.sbuf_tensor(name, shape, dt))

        K = sb("K", [P, NK], F32)
        ident = K[:, K_ID:K_ID + P]
        mask = K[:, K_MASK:K_MASK + 2 * P]
        Y = sb("Y", [P, NTT * C], F32)
        gu_raw = sb("gu_raw", [P, 2, 2 * NC * P], F32)
        wd_raw = sb("wd_raw", [P, 2, C], F32)
        mv = sb("mv", [P, NT, 8], F32)
        st = sb("st", [P, NT, 6], F32)

        ph1 = ctx.enter_context(ExitStack())
        WH = sb("WH", [P, 4, NC, C], F32R, ph1)
        WL = sb("WL", [P, 4, NC, C], F32R, ph1)
        QS = sb("QS", [P, 2, NT, NBLK * P], F32, ph1)
        w_raw = QS[:, :, :, :].rearrange("p a t (c n) -> p (a t) c n", c=NC)
        XR = sb("XR", [P, NC, T], F32, ph1)
        XH = sb("XH", [P, NC, T], F32R, ph1)
        XL = sb("XL", [P, NC, T], F32R, ph1)
        XN = sb("XN", [P, NT, C], F32, ph1)
        T1 = sb("T1", [P, 2, C], F32, ph1)
        RQ = sb("RQ", [P, 2, C], F32, ph1)
        V = sb("V", [P, NT, H, 32], F32, ph1)
        QKT = sb("QKT", [P, R_QKT, 2, T], F32R, ph1)
        SM = sb("SM", [P, R_SM, SW], F32, ph1)
        PR = sb("PR", [P, R_P, SW], F32, ph1)
        PTS = sb("PTS", [P, R_PTS, SW], F32, ph1)
        nb = sb("nb", [P, H, NT], F32, ph1)
        OT = sb("OT", [P, NG, T], F32, ph1)
        rden = sb("rden", [P, 4, H // 2], F32, ph1)
        ON = sb("ON", [P, NT, C], F32, ph1)
        OH = sb("OH", [P, NC, T], F32R, ph1)
        OL = sb("OL", [P, NC, T], F32R, ph1)
        RES = sb("RES", [P, NT, C], F32, ph1)
        ph1.close()

        YH = sb("YH", [P, NC, B * T], F32R)
        YL = sb("YL", [P, NC, B * T], F32R)
        GH = sb("GH", [P, 2, 2 * NC * P], F32R)
        GL = sb("GL", [P, 2, 2 * NC * P], F32R)
        DH = sb("DH", [P, NI, C], F32R)
        DL = sb("DL", [P, NI, C], F32R)
        IQ = sb("IQ", [P, NI * B * T], F32R)
        f_sil = sb("f_sil", [P, 2, HALF], F32)
        f_v = sb("f_v", [P, HALF], F32)
        f_c = sb("f_c", [P, HALF], F32)
        f_r = sb("f_r", [P, HALF], F32)
        f_d = sb("f_d", [P, HALF], F32)
        f_s = sb("f_s", [P, HALF], F32)
        f_e = sb("f_e", [P, HALF], F32)
        z = sb("z", [P, 2, C], F32)
        o = sb("o", [P, 2, C], F32)
        mz = sb("mz", [P, 2, 8], F32)
        sz = sb("sz", [P, 2, 6], F32)

        bank = [ctx.enter_context(nc.psum_tensor(f"bank{i}", [P, 512], F32)) for i in range(8)]
        bA, bTR, bS, bPT = bank[0:2], bank[2], bank[3:6], bank[6:8]
        bYT, bG, bU, bD = bank[0:2], bank[2:4], bank[4:6], bank[6:8]

        names = """k_in pool_tick dve_tick w_in0 w_in1 w_in2 w_in3 w_hi w_lo v_init xt_in xn_in xh xl proj t1 rope stack v_sb tr qkt sc sm pr pt pts pv ot
                   ob on oT oh ol yp res ln_dve ln_var ln_rstd y_out
                   yt yh yl gu_in0 gu_in1 wd_in0 wd_in1 gu_hi gu_lo wd_hi wd_lo g_mm u_mm sil f_dve f_r_ready f_sgn iq
                   dn d_sb o_dve o_r o_sgn z_var z_rstd z_out stored0 stored1""".split()
        S = {n: ctx.enter_context(nc.semaphore("s_" + n)) for n in names}
        block = ctx.enter_context(nc.Block())

        per = {e: A_USES.count(e) for e in ("dve", "act")}

        def a_reader(k):
            if k < V_USE:
                return "rope", k + 1, 4
            if k < AV_USE:
                return "v_sb", k - V_USE + 1, 2
            if k < Y_USE:
                return "ot", k - AV_USE + 1, NG
            return "res", k - Y_USE + 1, NT


        def heads_schedule():
            return range(H + LAG_AV)

        @block.sync
        def _(sp):
            sp.dma_start(K[:, :], consts).then_inc(S["k_in"], 16)
            with sp.Fori(0, B) as b:
                sp.wait_ge(S["xl"], b)
                sp.dma_start(XR[:, :, :], xT[bass.ds(b, 1)].rearrange("o (c p) t -> p (o c) t", p=P)).then_inc(S["xt_in"], 16)
                sp.wait_ge(S["res"], b * NT)
                sp.dma_start(XN[:, :, :], x[bass.ds(b, 1)].rearrange("o (t p) c -> p (o t) c", p=P)).then_inc(S["xn_in"], 16)

            def weights(i, slot, first):
                if not first:
                    sp.wait_ge(S["gu_lo"], i - 1)
                    sp.wait_ge(S["wd_lo"], i - 1)
                sp.dma_start(gu_raw[:, slot, :], wgu[bass.ds(i, 1)].rearrange("o p n -> p (o n)")).then_inc(S[f"gu_in{slot}"], 16)
                sp.dma_start(wd_raw[:, slot, :], wd[bass.ds(i, 1)].rearrange("o p n -> p (o n)")).then_inc(S[f"wd_in{slot}"], 16)

            weights(0, 0, True)
            weights(1, 1, True)
            with sp.Fori(2, NI - 1, 2) as i:
                weights(i, 0, False)
                weights(i + 1, 1, False)
            weights(NI - 1, 0, False)
            for t in range(NTT):
                sp.wait_ge(S["z_out"], t + 1)
                sp.dma_start(out[t * P:(t + 1) * P, :], o[:, t % 2, :]).then_inc(S[f"stored{t % 2}"], 16)
            for r in range(2):
                sp.wait_ge(S[f"stored{r}"], 16 * NTT // 2)

        @block.gpsimd
        def _(pool):
            for w in range(4):
                pool.dma_start(w_raw[:, w, :, :], wqkvo[w].rearrange("(c p) n -> p c n", p=P)).then_inc(S[f"w_in{w}"], 16)
            with pool.Fori(0, B) as b:
                pool.wait_ge(S["xh"], b + 1)
                nc.gpsimd.tensor_tensor(XL[:, :, :], XR[:, :, :], XH[:, :, :].bitcast(F32), ALU.subtract).then_inc(S["xl"], 1)
                for n in range(4):
                    a, t = divmod(n, NT)
                    pool.wait_ge(S["w_lo"], 4)
                    pool.wait_ge(S["rope"], b * 4 + n + 1)
                    pool.wait_ge(S["tr"], b * NBLK)
                    pool.sem_inc(S["pool_tick"], 1)
                    q = RQ[:, n % 2, :].rearrange("p (h d) -> p h d", d=D)
                    s = QS[:, a, t, :].rearrange("p (h k d) -> p h k d", k=4, d=D)
                    for k in (0, 1 if a == 0 else 2):
                        last = nc.gpsimd.tensor_copy(s[:, :, k, :].bitcast(F32R), q)
                    last.then_inc(S["stack"], 1)
                    pool.wait_ge(S["stack"], b * 8 + 2 * n + 1)
                    nc.gpsimd.tensor_tensor(s[:, :, 2 if a == 0 else 1, :], q, s[:, :, 0, :], ALU.subtract).then_inc(S["stack"], 1)
                for t in range(NT):
                    pool.wait_ge(S["ln_var"], b * NT + t + 1)
                    nc.gpsimd.tensor_tensor(mv[:, t, 3:4], mv[:, t, 2:3], K[:, K_HALF:K_HALF + 1], ALU.pow).then_inc(S["ln_rstd"], 1)

            pool.wait_ge(S["y_out"], NTT)

            def split(i, slot, first):
                pool.wait_ge(S["gu_hi"], i + 1)
                if not first:
                    pool.wait_ge(S["u_mm"], NHALF * (i - 1))
                nc.gpsimd.tensor_tensor(GL[:, slot, :], gu_raw[:, slot, :], GH[:, slot, :].bitcast(F32), ALU.subtract).then_inc(S["gu_lo"], 1)
                pool.wait_ge(S["wd_hi"], i + 1)
                at = bass.ds(i, 1)
                nc.gpsimd.tensor_tensor(DL[:, at, :].rearrange("p o n -> p (o n)"), wd_raw[:, slot, :],
                                        DH[:, at, :].rearrange("p o n -> p (o n)").bitcast(F32), ALU.subtract).then_inc(S["wd_lo"], 1)

            split(0, 0, True)
            split(1, 1, True)
            with pool.Fori(2, NI - 1, 2) as i:
                split(i, 0, False)
                split(i + 1, 1, False)
            split(NI - 1, 0, False)
            for t in range(NTT):
                pool.wait_ge(S["z_var"], t + 1)
                nc.gpsimd.tensor_tensor(mz[:, t % 2, 3:4], mz[:, t % 2, 2:3], K[:, K_HALF:K_HALF + 1], ALU.pow).then_inc(S["z_rstd"], 1)

        @block.scalar
        def _(act):
            for w in range(4):
                act.wait_ge(S[f"w_in{w}"], 16)
                nc.scalar.activation(WH[:, w, :, :], w_raw[:, w, :, :], ACT.Copy).then_inc(S["w_hi"], 1)
            act.wait_ge(S["k_in"], 16)
            with act.Fori(0, B) as b:
                act.wait_ge(S["xt_in"], b * 16 + 16)
                act.wait_ge(S["proj"], b * 6)
                nc.scalar.activation(XH[:, :, :], XR[:, :, :], ACT.Copy).then_inc(S["xh"], 1)
                for n in range(4):
                    a, t = divmod(n, NT)
                    act.wait_ge(S["proj"], b * 6 + n + 1)
                    act.wait_ge(S["rope"], b * 4 + max(n - 1, 0))
                    sin = K[:, K_ROT + 4 * t + 2 * a + 1:K_ROT + 4 * t + 2 * a + 2]
                    nc.scalar.activation(T1[:, n % 2, :], bA[n % 2][:, :], ACT.Copy, scale=sin).then_inc(S["t1"], 1)
                for t in range(NT):
                    act.wait_ge(S["proj"], b * 6 + 4 + t + 1)
                    act.wait_ge(S["v_init"], 2)
                    nc.scalar.activation(V[:, t, :, 0:D], bA[(V_USE + t) % 2][:, :].rearrange("p (h d) -> p h d", d=D),
                                         ACT.Copy).then_inc(S["v_sb"], 1)

                def qkt(j):
                    act.wait_ge(S["tr"], b * NBLK + j + 1)
                    act.wait_ge(S["sc"], b * H + max(2 * (j - R_QKT + 1), 0))
                    nc.scalar.activation(QKT[:, j % R_QKT, :, :], bTR[:, :].rearrange("p (a t) -> p a t", a=2),
                                         ACT.Copy).then_inc(S["qkt"], 1)

                def exps(h):
                    act.wait_ge(S["sm"], b * H + h + 1)
                    act.wait_ge(S["pt"], b * H + max(h - R_P + 1, 0))
                    for t in range(NT):
                        cols = slice(0, P) if t == 0 else slice(P, SW)
                        last = nc.scalar.activation(PR[:, h % R_P, cols], SM[:, h % R_SM, cols], ACT.Exp,
                                                    bias=nb[:, h, t:t + 1], scale=-1.0)
                    last.then_inc(S["pr"], 1)

                def ot(g):
                    act.wait_ge(S["pv"], b * H + 4 * (g + 1))
                    nc.scalar.activation(OT[:, g, :], bA[(AV_USE + g) % 2][:, 0:T], ACT.Copy).then_inc(S["ot"], 1)

                qkt(0)
                qkt(1)
                for s in heads_schedule():
                    if s % 2 == 0 and s // 2 + 2 < NBLK:
                        qkt(s // 2 + 2)
                    if s < H:
                        exps(s)
                    if s >= LAG_AV + 3 and (s - LAG_AV) % 4 == 3:
                        ot((s - LAG_AV) // 4)
                for k in range(2):
                    act.wait_ge(S["oT"], b * 2 + k + 1)
                    act.wait_ge(S["yp"], b * NT)
                    nc.scalar.activation(OH[:, 2 * k:2 * k + 2, :], bPT[k][:, :].rearrange("p (c t) -> p c t", c=2),
                                         ACT.Copy).then_inc(S["oh"], 1)

            act.wait_ge(S["y_out"], NTT)
            for t in range(NTT):
                act.wait_ge(S["yt"], t + 1)
                nc.scalar.activation(YH[:, :, t * P:(t + 1) * P], bYT[t % 2][:, :].rearrange("p (c t) -> p c t", c=NC),
                                     ACT.Copy).then_inc(S["yh"], 1)

            def split(i, slot, first):
                act.wait_ge(S[f"gu_in{slot}"], (i - slot) * 8 + 16)
                if not first:
                    act.wait_ge(S["u_mm"], NHALF * (i - 1))
                nc.scalar.activation(GH[:, slot, :], gu_raw[:, slot, :], ACT.Copy).then_inc(S["gu_hi"], 1)
                act.wait_ge(S[f"wd_in{slot}"], (i - slot) * 8 + 16)
                at = bass.ds(i, 1)
                nc.scalar.activation(DH[:, at, :].rearrange("p o n -> p (o n)"), wd_raw[:, slot, :], ACT.Copy).then_inc(S["wd_hi"], 1)

            def gate(i, half):
                act.wait_ge(S["g_mm"], NHALF * i + half + 1)
                nc.scalar.activation(f_sil[:, half, :], bG[half][:, :], ACT.Silu, scale=1.0 / 128).then_inc(S["sil"], 1)
                act.wait_ge(S["f_r_ready"], NHALF * i + half + 1)
                nc.scalar.activation(f_s[:, :], f_r[:, :], ACT.Sign).then_inc(S["f_sgn"], 1)

            split(0, 0, True)
            split(1, 1, True)
            with act.Fori(0, NI - 3, 2) as i:
                for u in range(2):
                    for half in range(NHALF):
                        gate(i + u, half)
                    split(i + u + 2, u, False)
            for half in range(NHALF):
                gate(NI - 3, half)
            split(NI - 1, 0, False)
            for i in (NI - 2, NI - 1):
                for half in range(NHALF):
                    gate(i, half)
            for t in range(NTT):
                act.wait_ge(S["dn"], t + 1)
                nc.scalar.activation(f_sil[:, t % 2, :], bD[t % 2][:, :], ACT.Copy, scale=128.0).then_inc(S["d_sb"], 1)
                act.wait_ge(S["o_r"], t + 1)
                nc.scalar.activation(f_s[:, :], f_r[:, :], ACT.Sign).then_inc(S["o_sgn"], 1)

        @block.vector
        def _(dve):
            nc.vector.memset(V[:, :, :, :], 0.0).then_inc(S["v_init"], 1)
            dve.wait_ge(S["v_init"], 1)
            nc.vector.memset(V[:, :, :, D:D + 1], 1.0).then_inc(S["v_init"], 1)
            for w in range(4):
                dve.wait_ge(S["w_hi"], w + 1)
                nc.vector.tensor_tensor(WL[:, w, :, :], w_raw[:, w, :, :], WH[:, w, :, :].bitcast(F32), ALU.subtract).then_inc(S["w_lo"], 1)
            dve.wait_ge(S["w_lo"], 4)
            nc.vector.memset(QS[:, :, :, :].rearrange("p a t (h k) -> p (a t h) k", k=SLOT)[:, :, KROWS:SLOT], 0.0).then_inc(S["v_init"], 1)
            dve.wait_ge(S["k_in"], 16)
            with dve.Fori(0, B) as b:
                for n in range(4):
                    a, t = divmod(n, NT)
                    dve.wait_ge(S["t1"], b * 4 + n + 1)
                    dve.wait_ge(S["stack"], b * 8 + 2 * max(n - 1, 0))
                    cos = K[:, K_ROT + 4 * t + 2 * a:K_ROT + 4 * t + 2 * a + 1]
                    src = bA[n % 2][:, :].rearrange("p (h e d) -> p h e d", e=2, d=D // 2)
                    sn = T1[:, n % 2, :].rearrange("p (h e d) -> p h e d", e=2, d=D // 2)
                    dst = RQ[:, n % 2, :].rearrange("p (h e d) -> p h e d", e=2, d=D // 2)
                    nc.vector.scalar_tensor_tensor(out=dst[:, :, 0, :], in0=src[:, :, 0, :], scalar=cos, in1=sn[:, :, 1, :],
                                                   op0=ALU.mult, op1=ALU.subtract)
                    nc.vector.scalar_tensor_tensor(out=dst[:, :, 1, :], in0=src[:, :, 1, :], scalar=cos, in1=sn[:, :, 0, :],
                                                   op0=ALU.mult, op1=ALU.add).then_inc(S["rope"], 1)

                def scores(h):
                    dve.wait_ge(S["sc"], b * H + h + 1)
                    dve.wait_ge(S["pr"], b * H + max(h - R_SM + 1, 0))
                    dve.sem_inc(S["dve_tick"], 1)
                    for t in range(NT):
                        cols = slice(0, P) if t == 0 else slice(P, SW)
                        m = mask[:, P:2 * P] if t == 0 else mask
                        last = nc.vector.tensor_tensor_reduce(out=SM[:, h % R_SM, cols], in0=bS[h % R_S][:, cols], in1=m, scale=1.0,
                                                              scalar=HUGE, op0=ALU.add, op1=ALU.min, accum_out=nb[:, h, t:t + 1])
                    last.then_inc(S["sm"], 1)

                def pts(h):
                    dve.wait_ge(S["pt"], b * H + h + 1)
                    dve.wait_ge(S["pv"], b * H + max(h - R_PTS + 1, 0))
                    nc.vector.tensor_copy(PTS[:, h % R_PTS, :], bPT[h % R_PT][:, 0:SW]).then_inc(S["pts"], 1)

                for s in heads_schedule():
                    if s < H:
                        scores(s)
                    if LAG_PT <= s < H + LAG_PT:
                        pts(s - LAG_PT)
                for u in range(4):
                    half, t = divmod(u, NT)
                    dve.wait_ge(S["ob"], b * 4 + u + 1)
                    src = bS[(H + u) % R_S][:, :].rearrange("p (h d) -> p h d", d=32)
                    nc.vector.reciprocal(rden[:, u, :].rearrange("p (h o) -> p h o", o=1), src[:, :, D:D + 1]).then_inc(S["on"], 1)
                    dve.wait_ge(S["on"], b * 8 + 2 * u + 1)
                    nc.vector.tensor_tensor(ON[:, t, half * (C // 2):(half + 1) * (C // 2)].rearrange("p (h d) -> p h d", d=D),
                                            src[:, :, 0:D], rden[:, u, :].rearrange("p (h o) -> p h o", o=1).broadcast_to((P, H // 2, D)),
                                            ALU.mult).then_inc(S["on"], 1)
                for k in range(2):
                    dve.wait_ge(S["oh"], b * 2 + k + 1)
                    nc.vector.tensor_tensor(OL[:, 2 * k:2 * k + 2, :], bPT[k][:, :].rearrange("p (c t) -> p c t", c=2),
                                            OH[:, 2 * k:2 * k + 2, :].bitcast(F32), ALU.subtract).then_inc(S["ol"], 1)
                dve.wait_ge(S["xn_in"], b * 16 + 16)
                for t in range(NT):
                    dve.wait_ge(S["yp"], b * NT + t + 1)
                    nc.vector.tensor_tensor(RES[:, t, :], bA[(Y_USE + t) % 2][:, :], XN[:, t, :], ALU.add).then_inc(S["res"], 1)
                    dve.wait_ge(S["res"], b * NT + t + 1)
                    nc.vector.bn_stats(st[:, t, :], RES[:, t, :]).then_inc(S["ln_dve"], 1)
                    dve.wait_ge(S["ln_dve"], b * 2 * NT + 2 * t + 1)
                    dve.sem_inc(S["dve_tick"], 1)
                    nc.vector.bn_aggr(mv[:, t, 0:2], st[:, t, :]).then_inc(S["ln_dve"], 1)
                    dve.wait_ge(S["ln_dve"], b * 2 * NT + 2 * t + 2)
                    nc.vector.tensor_scalar(mv[:, t, 2:3], mv[:, t, 1:2], EPS, None, ALU.add).then_inc(S["ln_var"], 1)
                for t in range(NT):
                    dve.wait_ge(S["ln_rstd"], b * NT + t + 1)
                    nc.vector.tensor_scalar(Y[:, bass.ds(b * (NT * C) + t * C, C)], RES[:, t, :], mv[:, t, 0:1], mv[:, t, 3:4],
                                            ALU.subtract, ALU.mult).then_inc(S["y_out"], 1)

            for t in range(NTT):
                dve.wait_ge(S["yh"], t + 1)
                nc.vector.tensor_tensor(YL[:, :, t * P:(t + 1) * P], bYT[t % 2][:, :].rearrange("p (c t) -> p c t", c=NC),
                                        YH[:, :, t * P:(t + 1) * P].bitcast(F32), ALU.subtract).then_inc(S["yl"], 1)

            def truncate(n, ready, sgn, sgn_value, chain, base, dst, v):
                k = [base]

                def link(ins):
                    ins.then_inc(chain, 1)
                    k[0] += 1
                    dve.wait_ge(chain, k[0])

                link(nc.vector.tensor_scalar(f_c[:, :], v, -128.0, 127.0, ALU.max, ALU.min))
                nc.vector.tensor_scalar(f_r[:, :], f_c[:, :], MAGIC, -MAGIC, ALU.add, ALU.add).then_inc(ready, 1)
                dve.wait_ge(ready, sgn_value)
                link(nc.vector.tensor_tensor(f_d[:, :], f_r[:, :], f_c[:, :], ALU.subtract))
                link(nc.vector.tensor_tensor(f_e[:, :], f_d[:, :], f_r[:, :], ALU.mult))
                dve.wait_ge(sgn, sgn_value)
                link(nc.vector.scalar_tensor_tensor(out=f_d[:, :], in0=f_e[:, :], scalar=0.0, in1=f_s[:, :], op0=ALU.is_gt, op1=ALU.mult))
                return nc.vector.tensor_tensor(dst, f_r[:, :], f_d[:, :], ALU.subtract)

            def inner(i, half):
                n = NHALF * i + half
                dve.wait_ge(S["sil"], n + 1)
                dve.wait_ge(S["u_mm"], n + 1)
                nc.vector.tensor_tensor(f_v[:, :], f_sil[:, half, :], bU[half][:, :], ALU.mult).then_inc(S["f_dve"], 1)
                dve.wait_ge(S["f_dve"], n * 5 + 1)
                at = i * (B * T) + half * HALF
                dst = IQ[:, bass.ds(at, HALF)]
                truncate(n, S["f_r_ready"], S["f_sgn"], n + 1, S["f_dve"], n * 5 + 1, dst, f_v[:, :]).then_inc(S["iq"], 1)

            with dve.Fori(0, NI - 1, 2) as i:
                for u in range(2):
                    for half in range(NHALF):
                        inner(i + u, half)
            for half in range(NHALF):
                inner(NI - 1, half)
            for t in range(NTT):
                dve.wait_ge(S["d_sb"], t + 1)
                base = t * 8
                r = t % 2
                truncate(t, S["o_r"], S["o_sgn"], t + 1, S["o_dve"], base, f_v[:, :], f_sil[:, r, :]).then_inc(S["o_dve"], 1)
                dve.wait_ge(S["o_dve"], base + 5)
                nc.vector.tensor_tensor(z[:, r, :], f_v[:, :], Y[:, t * C:(t + 1) * C], ALU.add).then_inc(S["o_dve"], 1)
                dve.wait_ge(S["o_dve"], base + 6)
                nc.vector.bn_stats(sz[:, r, :], z[:, r, :]).then_inc(S["o_dve"], 1)
                dve.wait_ge(S["o_dve"], base + 7)
                nc.vector.bn_aggr(mz[:, r, 0:2], sz[:, r, :]).then_inc(S["o_dve"], 1)
                dve.wait_ge(S["o_dve"], base + 8)
                nc.vector.tensor_scalar(mz[:, r, 2:3], mz[:, r, 1:2], EPS, None, ALU.add).then_inc(S["z_var"], 1)
                dve.wait_ge(S["z_rstd"], t + 1)
                if t >= 2:
                    dve.wait_ge(S[f"stored{r}"], 16 * (t // 2))
                nc.vector.tensor_scalar(o[:, r, :], z[:, r, :], mz[:, r, 0:1], mz[:, r, 3:4], ALU.subtract, ALU.mult).then_inc(S["z_out"], 1)

        @block.tensor
        def _(pe):
            def three(dst, ah, al, bh, bl, n):
                for c in range(n):
                    nc.tensor.matmul(dst, ah(c), bh(c), start=(c == 0), stop=False)
                    nc.tensor.matmul(dst, ah(c), bl(c), start=False, stop=False)
                    last = nc.tensor.matmul(dst, al(c), bh(c), start=False, stop=(c == n - 1))
                return last

            pe.wait_ge(S["k_in"], 16)
            pe.wait_ge(S["v_init"], 3)
            with pe.Fori(0, B) as b:
                def a_free(k):
                    if k >= R_A:
                        name, count, per_b = a_reader(k - R_A)
                        pe.wait_ge(S[name], b * per_b + count)
                    else:
                        pe.wait_ge(S["res"], b * NT)

                pe.wait_ge(S["xh"], b + 1)
                pe.wait_ge(S["xl"], b + 1)
                for n in range(6):
                    w, t = divmod(n, NT)
                    a_free(n)
                    pe.wait_ge(S["w_lo"], w + 1)
                    tok = slice(t * P, (t + 1) * P)
                    three(bA[n % 2][:, :], lambda c: XH[:, c, tok], lambda c: XL[:, c, tok],
                          lambda c: WH[:, w, c, :], lambda c: WL[:, w, c, :], NC).then_inc(S["proj"], 1)

                def stack_t(j):
                    if j == 0:
                        pe.wait_ge(S["stack"], b * 8 + 8)
                    pe.wait_ge(S["qkt"], b * NBLK + j)
                    for a in range(2):
                        for t in range(NT):
                            last = nc.tensor.transpose(bTR[:, a * T + t * P:a * T + (t + 1) * P], QS[:, a, t, j * P:(j + 1) * P], ident)
                    last.then_inc(S["tr"], 1)

                def scores(h):
                    j, half = divmod(h, 2)
                    rows = slice(half * SLOT, half * SLOT + KROWS)
                    pe.wait_ge(S["qkt"], b * NBLK + j + 1)
                    pe.wait_ge(S["sm"], b * H + max(h - R_S + 1, 0))
                    if h < R_S:
                        pe.wait_ge(S["on"], b * 8)
                    q = QKT[rows, j % R_QKT, 0, :]
                    k = QKT[rows, j % R_QKT, 1, :]
                    nc.tensor.matmul(bS[h % R_S][:, 0:P], q[:, 0:P], k[:, 0:P], start=True, stop=True)
                    nc.tensor.matmul(bS[h % R_S][:, P:SW], q[:, P:T], k[:, 0:T], start=True, stop=True).then_inc(S["sc"], 1)

                def probs_t(h):
                    pe.wait_ge(S["pr"], b * H + h + 1)
                    pe.wait_ge(S["pts"], b * H + max(h - R_PT + 1, 0))
                    if h < R_PT:
                        pe.wait_ge(S["ol"], b * 2)
                    for i in range(3):
                        last = nc.tensor.transpose(bPT[h % R_PT][:, i * P:(i + 1) * P], PR[:, h % R_P, i * P:(i + 1) * P], ident)
                    last.then_inc(S["pt"], 1)

                def pv(h):
                    g, r = divmod(h, 4)
                    if r == 0:
                        a_free(AV_USE + g)
                    pe.wait_ge(S["pts"], b * H + h + 1)
                    if h == 0:
                        pe.wait_ge(S["v_sb"], b * 2 + 2)
                    dst = bA[(AV_USE + g) % 2][32 * r:32 * r + 32, 0:T]
                    p = PTS[:, h % R_PTS, :]
                    nc.tensor.matmul(dst, V[:, 0, h, :], p[:, 0:T], start=True, stop=False)
                    nc.tensor.matmul(dst[:, P:T], V[:, 1, h, :], p[:, T:SW], start=False, stop=True).then_inc(S["pv"], 1)

                stack_t(0)
                stack_t(1)
                for s in heads_schedule():
                    if s % 2 == 0 and s // 2 + 2 < NBLK:
                        stack_t(s // 2 + 2)
                    if s < H:
                        scores(s)
                    if LAG_PT <= s < H + LAG_PT:
                        probs_t(s - LAG_PT)
                    if s >= LAG_AV:
                        pv(s - LAG_AV)
                for u in range(4):
                    half, t = divmod(u, NT)
                    pe.wait_ge(S["ot"], b * NG + (half + 1) * (NG // 2))
                    pe.wait_ge(S["sm"], b * H + H)
                    if u >= R_S:
                        pe.wait_ge(S["on"], b * 8 + 2 * (u - R_S + 1))
                    for g in range(NG // 2):
                        last = nc.tensor.transpose(bS[(H + u) % R_S][:, g * P:(g + 1) * P],
                                                   OT[:, half * (NG // 2) + g, t * P:(t + 1) * P], ident)
                    last.then_inc(S["ob"], 1)
                for k in range(2):
                    pe.wait_ge(S["on"], b * 8 + 4 * (k + 1))
                    pe.wait_ge(S["pts"], b * H + H)
                    for i in range(2):
                        for t in range(NT):
                            c = 2 * k + i
                            last = nc.tensor.transpose(bPT[k][:, i * T + t * P:i * T + (t + 1) * P], ON[:, t, c * P:(c + 1) * P], ident)
                    last.then_inc(S["oT"], 1)
                pe.wait_ge(S["ol"], b * 2 + 2)
                for t in range(NT):
                    a_free(Y_USE + t)
                    tok = slice(t * P, (t + 1) * P)
                    three(bA[(Y_USE + t) % 2][:, :], lambda c: OH[:, c, tok], lambda c: OL[:, c, tok],
                          lambda c: WH[:, 3, c, :], lambda c: WL[:, 3, c, :], NC).then_inc(S["yp"], 1)

            pe.wait_ge(S["res"], NTT)
            for t in range(NTT):
                pe.wait_ge(S["y_out"], t + 1)
                if t >= 2:
                    pe.wait_ge(S["yl"], t - 1)
                for c in range(NC):
                    last = nc.tensor.transpose(bYT[t % 2][:, c * P:(c + 1) * P], Y[:, t * C + c * P:t * C + (c + 1) * P], ident)
                last.then_inc(S["yt"], 1)

            def up(i, slot, first):
                pe.wait_ge(S["gu_lo"], i + 1)
                for half in range(NHALF):
                    n = NHALF * i + half
                    tok = slice(half * HALF, (half + 1) * HALF)
                    if first:
                        pe.wait_ge(S["yl"], (half + 1) * NTT // NHALF)
                    for k, (dst, done, read) in enumerate(((bG, "g_mm", "sil"), (bU, "u_mm", "f_r_ready"))):
                        if not first:
                            pe.wait_ge(S[read], n - 1)
                        w = [m[:, slot, :].rearrange("p (k c n) -> p k c n", k=2, c=NC) for m in (GH, GL)]
                        three(dst[half][:, :], lambda c: w[0][:, k, c, :], lambda c: w[1][:, k, c, :],
                              lambda c: YH[:, c, tok], lambda c: YL[:, c, tok], NC).then_inc(S[done], 1)

            up(0, 0, True)
            up(1, 1, False)
            with pe.Fori(2, NI - 1, 2) as i:
                up(i, 0, False)
                up(i + 1, 1, False)
            up(NI - 1, 0, False)
            pe.wait_ge(S["iq"], NHALF * NI)
            pe.wait_ge(S["wd_lo"], NI)
            for t in range(NTT):
                if t >= 2:
                    pe.wait_ge(S["d_sb"], t - 1)
                for i in range(NI):
                    a = IQ[:, i * B * T + t * P:i * B * T + (t + 1) * P]
                    nc.tensor.matmul(bD[t % 2][:, :], a, DH[:, i, :], start=(i == 0), stop=False)
                    last = nc.tensor.matmul(bD[t % 2][:, :], a, DL[:, i, :], start=False, stop=(i == NI - 1))
                last.then_inc(S["dn"], 1)


def kernel(**inputs):
    import numpy as np
    import concourse.bacc as bacc
    from concourse.bass_utils import run_bass_kernel_spmd

    def pairs_apart(w):
        return w.reshape(H, D // 2, 2, C).transpose(0, 2, 1, 3).reshape(C, C)

    def padded(w):
        return np.concatenate([w, np.zeros((NI * P - INTER, C), w.dtype)])

    a = {k: np.asarray(v) for k, v in inputs.items()}
    xs = a["L0_attn_x"]
    wqkvo = np.stack([pairs_apart(a["L0_attn_wq"]).T, pairs_apart(a["L0_attn_wk"]).T, a["L0_attn_wv"].T, a["L0_attn_wo"].T])
    gu = np.stack([padded(a["L0_ffn_w_gate"]), padded(a["L0_ffn_w_up"])])
    gu = gu.reshape(2, NI, P, NC, P).transpose(1, 4, 0, 3, 2).reshape(NI, P, 2 * NC * P)
    wd = padded(a["L0_ffn_w_down"].T).reshape(NI, P, C)

    k = np.zeros((P, NK), np.float32)
    k[:, K_ID:K_ID + P] = np.eye(P)
    k[:, K_MASK + P:K_MASK + 2 * P] = np.triu(np.full((P, P), BIG), 1)
    theta = np.arange(T, dtype=np.float32).reshape(NT, P)
    for t in range(NT):
        for j, v in enumerate((-D ** -0.5 * np.cos(theta[t]), -D ** -0.5 * np.sin(theta[t]), np.cos(theta[t]), np.sin(theta[t]))):
            k[:, K_ROT + 4 * t + j] = v
    k[:, K_HALF] = -0.5

    nc = bacc.Bacc("TRN2", target_bir_lowering=False, num_devices=1)
    arrays, args = {}, []
    for name, v in (("xT", xs.transpose(0, 2, 1)), ("x", xs), ("wqkvo", wqkvo), ("wgu", gu), ("wd", wd), ("consts", k)):
        v = np.ascontiguousarray(v)
        arrays[name] = v
        args.append(nc.dram_tensor(name, v.shape, mybir.dt.from_np(v.dtype), kind="ExternalInput").ap())
    args.append(nc.dram_tensor("out", (B * T, C), F32, kind="ExternalOutput").ap())
    layer(nc, *args)
    r = run_bass_kernel_spmd(nc, [arrays], core_ids=[0])
    return r.results[0]["out"].reshape(B, T, C)
```

```python
import concourse.bass as bass
from concourse import mybir
from contextlib import ExitStack

F32 = mybir.dt.float32
F32R = mybir.dt.float32r
ALU = mybir.AluOpType
ACT = mybir.ActivationFunctionType

P = 128
B, T, C, H, D = 4, 256, 512, 32, 16
INTER = 1376
NI = -(-INTER // P)
NT = T // P
NTT = B * NT
NC = C // P
NBLK = H // 2
NG = H // 4
SLOT = 64
KROWS = 3 * D
SW = 3 * P
BIG = 1.0e30
HUGE = 3.0e38
MAGIC = 1.5 * 2.0 ** 23
EPS = 1e-5
HALF = 512
NHALF = B * T // HALF

K_ID = 0
K_MASK = K_ID + P
K_ROT = K_MASK + 2 * P
K_HALF = K_ROT + 4 * NT
NK = K_HALF + 1

R_S, R_PT, R_QKT, R_SM, R_P, R_PTS, R_RQ = 2, 2, 3, 3, 3, 7, 3
LAG_PT, LAG_AV = 3, 5
STEPS = H + LAG_AV

PREV = [("back", 2, -1, 1, 1, 1), ("back", 3, -1, 0, 2, 1), ("chan", 1, -1, 1, 4, 1),
        ("outp", 0, -1, 0, 6, NC), ("outp", 1, -1, 1, 10, NC)]
OWN = [("back", 0, 0, 0, 22, 1), ("back", 1, 0, 0, 24, 1), ("chan", 0, 0, 0, 26, 1)]
NEXT = [("proj", 0, 1, 0, 14, NC), ("proj", 1, 1, 1, 18, NC), ("proj", 2, 1, 1, 23, NC),
        ("proj", 3, 1, 0, 28, NC), ("proj", 4, 1, 1, 30, NC), ("proj", 5, 1, 0, 33, NC)]
FFN0 = [("yt", 0, 0, 1, 16, 1), ("yt", 1, 0, 0, 18, 1), ("yt", 2, 0, 1, 20, 1), ("yt", 3, 0, 0, 28, 1)]


def by_step(items):
    return sorted(items, key=lambda x: x[4])


SHARED = {
    "before": NEXT,
    "first": by_step(OWN + NEXT),
    "middle": by_step(PREV + OWN + NEXT),
    "last": by_step(PREV + OWN + FFN0),
    "after": PREV,
}
BEFORE = {"first": "before", "middle": "middle", "last": "middle", "after": "last"}
HI_STEP = {28: 0, 29: 1, 30: 2, 33: 3}


def layer(nc, xT, x, wqkvo, wgu, wd, consts, out):
    ctx = ExitStack()
    with ctx:
        def sb(name, shape, dt, where=ctx):
            return where.enter_context(nc.sbuf_tensor(name, shape, dt))

        K = sb("K", [P, NK], F32)
        ident = K[:, K_ID:K_ID + P]
        mask = K[:, K_MASK:K_MASK + 2 * P]
        Y = sb("Y", [P, NTT * C], F32)
        gu_raw = sb("gu_raw", [P, 2, 2 * NC * P], F32)
        wd_raw = sb("wd_raw", [P, 2, C], F32)

        identr = sb("identr", [P, P], F32R)

        ph1 = ctx.enter_context(ExitStack())
        WQH = sb("WQH", [P, 3, NC, C], F32R, ph1)
        WQL = sb("WQL", [P, 3, NC, C], F32R, ph1)
        WOH = sb("WOH", [P, NC, C], F32R, ph1)
        WOL = sb("WOL", [P, NC, C], F32R, ph1)
        with ExitStack() as ph0:
            w_raw = sb("w_raw", [P, 4, NC, C], F32, ph0)
        QS = sb("QS", [P, 2, NT, NBLK * P], F32R, ph1)
        XR = sb("XR", [P, NC, T], F32, ph1)
        XH = sb("XH", [P, NC, T], F32R, ph1)
        XL = sb("XL", [P, NC, T], F32R, ph1)
        RES = sb("RES", [P, NT, C], F32, ph1)
        T1 = sb("T1", [P, 2, C], F32, ph1)
        RQ = sb("RQ", [P, R_RQ, C], F32, ph1)
        V = sb("V", [P, NT, H, 32], F32, ph1)
        QKT = sb("QKT", [P, R_QKT, 2, T], F32R, ph1)
        SM = sb("SM", [P, R_SM, SW], F32, ph1)
        PR = sb("PR", [P, R_P, SW], F32, ph1)
        PTS = sb("PTS", [P, R_PTS, SW], F32, ph1)
        nb = sb("nb", [P, H, NT], F32, ph1)
        OT = sb("OT", [P, NG, T], F32, ph1)
        rden = sb("rden", [P, 4, H // 2], F32, ph1)
        ON = sb("ON", [P, NT, C], F32, ph1)
        OH = sb("OH", [P, NC, T], F32R, ph1)
        OL = sb("OL", [P, NC, T], F32R, ph1)
        mv = sb("mv", [P, NT, 8], F32, ph1)
        st = sb("st", [P, NT, 6], F32, ph1)
        ph1.close()

        GH = sb("GH", [P, 2, 2 * NC * P], F32R)
        GL = sb("GL", [P, 2, 2 * NC * P], F32R)
        YH = [sb("YH0", [P, NC, HALF], F32R)]
        YL = [sb("YL0", [P, NC, HALF], F32R)]
        YH.append(sb("YH1", [P, NC, HALF], F32R))
        YL.append(sb("YL1", [P, NC, HALF], F32R))
        DH = sb("DH", [P, NI, C], F32R)
        DL = sb("DL", [P, NI, C], F32R)
        IQ = sb("IQ", [P, NI * B * T], F32R)
        f_sil = sb("f_sil", [P, 2, HALF], F32)
        f_v = sb("f_v", [P, HALF], F32)
        f_c = sb("f_c", [P, 2, HALF], F32)
        f_r = sb("f_r", [P, 2, HALF], F32)
        f_d = sb("f_d", [P, 2, HALF], F32)
        f_s = sb("f_s", [P, 2, HALF], F32)
        f_e = sb("f_e", [P, 2, HALF], F32)
        z = sb("z", [P, 2, C], F32)
        o = sb("o", [P, 2, C], F32)
        mz = sb("mz", [P, 2, 8], F32)
        sz = sb("sz", [P, 2, 6], F32)

        bank = [ctx.enter_context(nc.psum_tensor(f"bank{i}", [P, 512], F32)) for i in range(8)]
        bJ, bAV, bTR, bS, bPT = bank[0:2], bank[2], bank[3], bank[4:6], bank[6:8]
        bD, bG, bU = bank[2:4], bank[4:6], bank[6:8]

        names = """k_in identr pool_tick dve_tick w_in0 w_in1 w_in2 w_in3 w_hi w_lo v_init pads xt_in xn_in xh xl
                   proj t1 rope hi lo v_sb tr qkt sc sm pr pt pts pv ot ob rd on oT oh ol yp res ln_dve ln_var
                   ln_rstd y_out yt yh yl gu_in0 gu_in1 wd_in0 wd_in1 gu_hi gu_lo wd_hi wd_lo g_mm u_mm sil f_dve
                   f_round f_sgn iq dn d_sb o_clip o_round o_sgn o_pool o_dve z_var z_rstd z_out
                   stored0 stored1""".split()
        S = {n: ctx.enter_context(nc.semaphore("s_" + n)) for n in names}
        block = ctx.enter_context(nc.Block())

        def wait(eng, name, value):
            if not (isinstance(value, int) and value <= 0):
                eng.wait_ge(S[name], value)

        def rounds(eng, run):
            run(-1, "before")
            run(0, "first")
            with eng.Fori(1, B - 1) as b:
                run(b, "middle")
            run(B - 1, "last")
            run(B, "after")

        def steps(kind):
            return range(STEPS) if kind in ("first", "middle", "last") else range(0)

        def finished(kind, s):
            return [i for i in SHARED[kind] if i[4] + i[5] == s]


        @block.sync
        def _(sp):
            def load_xt(b):
                wait(sp, "xl", b)
                sp.dma_start(XR[:, :, :], xT[bass.ds(b, 1)].rearrange("o (c p) t -> p (o c) t", p=P)).then_inc(S["xt_in"], 16)

            def load_xn(b):
                wait(sp, "y_out", b * NT)
                sp.dma_start(RES[:, :, :], x[bass.ds(b, 1)].rearrange("o (t p) c -> p (o t) c", p=P)).then_inc(S["xn_in"], 16)

            load_xt(0)
            for w in range(4):
                sp.dma_start(w_raw[:, w, :, :], wqkvo[w].rearrange("(c p) n -> p c n", p=P)).then_inc(S[f"w_in{w}"], 16)
                if w == 0:
                    sp.dma_start(K[:, :], consts).then_inc(S["k_in"], 16)
            load_xt(1)
            load_xn(0)
            with sp.Fori(2, B) as b:
                load_xt(b)
                load_xn(b - 1)
            load_xn(B - 1)

            def weights(i, slot):
                wait(sp, "gu_lo", i - 1)
                sp.dma_start(gu_raw[:, slot, :], wgu[bass.ds(i, 1)].rearrange("o p n -> p (o n)")).then_inc(S[f"gu_in{slot}"], 16)
                wait(sp, "wd_lo", i - 1)
                sp.dma_start(wd_raw[:, slot, :], wd[bass.ds(i, 1)].rearrange("o p n -> p (o n)")).then_inc(S[f"wd_in{slot}"], 16)

            weights(0, 0)
            weights(1, 1)
            with sp.Fori(2, NI - 1, 2) as i:
                weights(i, 0)
                weights(i + 1, 1)
            weights(NI - 1, 0)
            for t in range(NTT):
                sp.wait_ge(S["z_out"], t + 1)
                sp.dma_start(out[t * P:(t + 1) * P, :], o[:, t % 2, :]).then_inc(S[f"stored{t % 2}"], 16)
            for r in range(2):
                sp.wait_ge(S[f"stored{r}"], 16 * NTT // 2)

        @block.gpsimd
        def _(pool):
            nc.gpsimd.memset(V[:, :, :, :], 0.0).then_inc(S["v_init"], 1)
            pool.wait_ge(S["v_init"], 1)
            nc.gpsimd.memset(V[:, :, :, D:D + 1], 1.0).then_inc(S["v_init"], 1)

            def split_gu(i, slot):
                pool.wait_ge(S["gu_hi"], i + 1)
                nc.gpsimd.tensor_tensor(GL[:, slot, :], gu_raw[:, slot, :], GH[:, slot, :].bitcast(F32), ALU.subtract).then_inc(S["gu_lo"], 1)

            def split_wd(i, slot):
                pool.wait_ge(S["wd_hi"], i + 1)
                at = bass.ds(i, 1)
                nc.gpsimd.tensor_tensor(DL[:, at, :].rearrange("p o n -> p (o n)"), wd_raw[:, slot, :],
                                        DH[:, at, :].rearrange("p o n -> p (o n)").bitcast(F32), ALU.subtract).then_inc(S["wd_lo"], 1)

            def run(b, kind):
                if kind in ("middle", "last", "after"):
                    for t in range(NT):
                        pool.wait_ge(S["ln_var"], (b - 1) * NT + t + 1)
                        nc.gpsimd.tensor_tensor(mv[:, t, 3:4], mv[:, t, 2:3], K[:, K_HALF:K_HALF + 1], ALU.pow).then_inc(S["ln_rstd"], 1)
                if kind in ("before", "first", "middle"):
                    n = b + 1
                    pool.wait_ge(S["xh"], n + 1)
                    nc.gpsimd.tensor_tensor(XL[:, :, :], XR[:, :, :], XH[:, :, :].bitcast(F32), ALU.subtract).then_inc(S["xl"], 1)
                    for m in range(4):
                        a, t = divmod(m, NT)
                        pool.wait_ge(S["hi"], n * 4 + m + 1)
                        q = RQ[:, m % R_RQ, :].rearrange("p (h d) -> p h d", d=D)
                        s = QS[:, a, t, :].rearrange("p (h k d) -> p h k d", k=4, d=D)
                        nc.gpsimd.tensor_tensor(s[:, :, 2 - a, :], q, s[:, :, 0, :].bitcast(F32), ALU.subtract).then_inc(S["lo"], 1)
                if kind == "last":
                    split_gu(0, 0)
                    split_gu(1, 1)

            rounds(pool, run)

            split_wd(0, 0)
            split_wd(1, 1)
            with pool.Fori(2, NI - 1, 2) as i:
                for u in range(2):
                    split_gu(i + u, u)
                    split_wd(i + u, u)
            split_gu(NI - 1, 0)
            split_wd(NI - 1, 0)

            def rest(t):
                r = t % 2
                pool.wait_ge(S["o_round"], t + 1)
                nc.gpsimd.tensor_tensor(f_d[:, r, :], f_r[:, r, :], f_c[:, r, :], ALU.subtract).then_inc(S["o_pool"], 1)
                pool.wait_ge(S["o_pool"], 2 * t + 1)
                nc.gpsimd.tensor_tensor(f_e[:, r, :], f_d[:, r, :], f_r[:, r, :], ALU.mult).then_inc(S["o_pool"], 1)

            rest(0)
            for t in range(NTT):
                if t + 1 < NTT:
                    rest(t + 1)
                pool.wait_ge(S["z_var"], t + 1)
                nc.gpsimd.tensor_tensor(mz[:, t % 2, 3:4], mz[:, t % 2, 2:3], K[:, K_HALF:K_HALF + 1], ALU.pow).then_inc(S["z_rstd"], 1)

        @block.scalar
        def _(act):
            def w_hi(w):
                act.wait_ge(S[f"w_in{w}"], 16)
                nc.scalar.activation(WQH[:, w, :, :] if w < 3 else WOH[:, :, :], w_raw[:, w, :, :], ACT.Copy).then_inc(S["w_hi"], 1)

            def x_hi(n):
                act.wait_ge(S["xt_in"], n * 16 + 16)
                wait(act, "proj", n * 6)
                nc.scalar.activation(XH[:, :, :], XR[:, :, :], ACT.Copy).then_inc(S["xh"], 1)

            def sine(n, m, bank):
                a, t = divmod(m, NT)
                act.wait_ge(S["proj"], n * 6 + m + 1)
                wait(act, "rope", n * 4 + m - 1)
                sin = K[:, K_ROT + 4 * t + 2 * a + 1:K_ROT + 4 * t + 2 * a + 2]
                nc.scalar.activation(T1[:, m % 2, :], bJ[bank][:, :], ACT.Copy, scale=sin).then_inc(S["t1"], 1)

            def values(n, t, bank):
                act.wait_ge(S["proj"], n * 6 + 4 + t + 1)
                wait(act, "pv", n * NG)
                act.wait_ge(S["v_init"], 2)
                nc.scalar.activation(V[:, t, :, 0:D], bJ[bank][:, :].rearrange("p (h d) -> p h d", d=D), ACT.Copy).then_inc(S["v_sb"], 1)

            def high(n, m):
                a, t = divmod(m, NT)
                act.wait_ge(S["rope"], n * 4 + m + 1)
                wait(act, "tr", n * NBLK)
                act.wait_ge(S["w_lo"], 4)
                q = RQ[:, m % R_RQ, :].rearrange("p (h o d) -> p h o d", o=1, d=D).broadcast_to((P, H, 2, D))
                s = QS[:, a, t, :].rearrange("p (h k d) -> p h k d", k=4, d=D)
                s = s[:, :, 0:2, :] if a == 0 else s[:, :, 0:3:2, :]
                nc.scalar.activation(s, q, ACT.Copy).then_inc(S["hi"], 1)

            def qkt(b, j):
                act.wait_ge(S["tr"], b * NBLK + j + 1)
                wait(act, "sc", b * H + max(2 * (j - R_QKT + 1), 0))
                nc.scalar.activation(QKT[:, j % R_QKT, :, :], bTR[:, :].rearrange("p (a t) -> p a t", a=2), ACT.Copy).then_inc(S["qkt"], 1)

            def exps(b, h):
                act.wait_ge(S["sm"], b * H + h + 1)
                wait(act, "pt", b * H + max(h - R_P + 1, 0))
                for t in range(NT):
                    cols = slice(0, P) if t == 0 else slice(P, SW)
                    last = nc.scalar.activation(PR[:, h % R_P, cols], SM[:, h % R_SM, cols], ACT.Exp, bias=nb[:, h, t:t + 1], scale=-1.0)
                last.then_inc(S["pr"], 1)

            def pv_out(b, g):
                act.wait_ge(S["pv"], b * NG + g + 1)
                wait(act, "ob", b * 4)
                nc.scalar.activation(OT[:, g, :], bAV[:, 0:T], ACT.Copy).then_inc(S["ot"], 1)

            def chan_hi(n, k, bank):
                act.wait_ge(S["oT"], n * 2 + k + 1)
                wait(act, "yp", n * NT)
                nc.scalar.activation(OH[:, 2 * k:2 * k + 2, :], bJ[bank][:, :].rearrange("p (c t) -> p c t", c=2), ACT.Copy).then_inc(S["oh"], 1)

            def y_hi(t, bank):
                half, r = divmod(t, NTT // NHALF)
                act.wait_ge(S["yt"], t + 1)
                nc.scalar.activation(YH[half][:, :, r * P:(r + 1) * P], bJ[bank][:, :].rearrange("p (c t) -> p c t", c=NC), ACT.Copy).then_inc(S["yh"], 1)

            def shared(b, item):
                kind, n, rel, bank, _, _ = item
                if kind == "proj" and n < 4:
                    sine(b + rel, n, bank)
                elif kind == "proj":
                    values(b + rel, n - 4, bank)
                elif kind == "chan":
                    chan_hi(b + rel, n, bank)
                elif kind == "yt":
                    y_hi(n, bank)

            def split_gu(i, slot, used):
                act.wait_ge(S[f"gu_in{slot}"], (i - slot) * 8 + 16)
                wait(act, "u_mm", used)
                nc.scalar.activation(GH[:, slot, :], gu_raw[:, slot, :], ACT.Copy).then_inc(S["gu_hi"], 1)

            def split_wd(i, slot):
                act.wait_ge(S[f"wd_in{slot}"], (i - slot) * 8 + 16)
                nc.scalar.activation(DH[:, bass.ds(i, 1), :].rearrange("p o n -> p (o n)"), wd_raw[:, slot, :], ACT.Copy).then_inc(S["wd_hi"], 1)

            def run(b, kind):
                if kind == "before":
                    x_hi(0)
                    w_hi(0)
                    act.wait_ge(S["k_in"], 16)
                    nc.scalar.activation(identr[:, :], ident, ACT.Copy).then_inc(S["identr"], 1)
                    w_hi(1)
                    sine(0, 0, 0)
                    sine(0, 1, 1)
                    w_hi(2)
                    sine(0, 2, 1)
                    w_hi(3)
                    high(0, 0)
                    sine(0, 3, 0)
                    for m in range(1, 4):
                        high(0, m)
                    values(0, 0, 1)
                    values(0, 1, 0)
                    return
                if kind == "after":
                    return
                qkt(b, 0)
                qkt(b, 1)
                for s in steps(kind):
                    if s % 2 == 0 and s // 2 + 2 < NBLK:
                        qkt(b, s // 2 + 2)
                    if s < H:
                        exps(b, s)
                    if s >= LAG_AV + 3 and (s - LAG_AV) % 4 == 3:
                        pv_out(b, (s - LAG_AV) // 4)
                    for item in finished(kind, s):
                        shared(b, item)
                    if kind != "last":
                        if s == 3:
                            x_hi(b + 1)
                        if s in HI_STEP:
                            high(b + 1, HI_STEP[s])
                    elif s in (24, 30):
                        split_gu(int(s == 30), int(s == 30), 0)
                for item in finished(kind, STEPS):
                    shared(b, item)

            rounds(act, run)

            def silu(n, slot):
                act.wait_ge(S["g_mm"], n + 1)
                nc.scalar.activation(f_sil[:, slot, :], bG[slot][:, :], ACT.Silu, scale=1.0 / 128).then_inc(S["sil"], 1)

            def sign(n):
                act.wait_ge(S["f_round"], n + 1)
                nc.scalar.activation(f_s[:, 0, :], f_r[:, 0, :], ACT.Sign).then_inc(S["f_sgn"], 1)

            silu(0, 0)
            chan_hi(B - 1, 1, 1)
            silu(1, 1)
            act.wait_ge(S["y_out"], NTT)
            split_wd(0, 0)
            split_wd(1, 1)
            for t in range(NTT // 2, NTT):
                y_hi(t, t % 2)
            sign(0)
            sign(1)
            for n in (2, 3):
                silu(n, n % 2)
                sign(n)
                split_gu(n, n % 2, n + 1)
                split_wd(n, n % 2)
            with act.Fori(4, NI - 1, 2) as i:
                for u in range(2):
                    for half in range(NHALF):
                        silu(NHALF * (i + u - 2) + half, half)
                        sign(NHALF * (i + u - 2) + half)
                    split_gu(i + u, u, NHALF * (i + u - 1))
                    split_wd(i + u, u)
            for i in (NI - 3, NI - 2, NI - 1):
                for half in range(NHALF):
                    silu(NHALF * i + half, half)
                    sign(NHALF * i + half)
                if i == NI - 3:
                    split_gu(NI - 1, 0, NHALF * (NI - 2))
                    split_wd(NI - 1, 0)
            for t in range(NTT):
                r = t % 2
                act.wait_ge(S["dn"], t + 1)
                if t >= 2:
                    act.wait_ge(S["o_clip"], t - 1)
                nc.scalar.activation(f_sil[:, r, :], bD[r][:, :], ACT.Copy, scale=128.0).then_inc(S["d_sb"], 1)
                act.wait_ge(S["o_round"], t + 1)
                if t >= 2:
                    act.wait_ge(S["z_var"], t - 1)
                nc.scalar.activation(f_s[:, r, :], f_r[:, r, :], ACT.Sign).then_inc(S["o_sgn"], 1)

        @block.vector
        def _(dve):
            def w_lo(w):
                dve.wait_ge(S["w_hi"], w + 1)
                hi, lo = (WQH[:, w, :, :], WQL[:, w, :, :]) if w < 3 else (WOH[:, :, :], WOL[:, :, :])
                nc.vector.tensor_tensor(lo, w_raw[:, w, :, :], hi.bitcast(F32), ALU.subtract).then_inc(S["w_lo"], 1)

            def rotate(n, m, bank):
                a, t = divmod(m, NT)
                dve.wait_ge(S["t1"], n * 4 + m + 1)
                wait(dve, "lo", n * 4 + max(m - R_RQ + 1, 0))
                cos = K[:, K_ROT + 4 * t + 2 * a:K_ROT + 4 * t + 2 * a + 1]
                src = bJ[bank][:, :].rearrange("p (h e d) -> p h e d", e=2, d=D // 2)
                sn = T1[:, m % 2, :].rearrange("p (h e d) -> p h e d", e=2, d=D // 2)
                dst = RQ[:, m % R_RQ, :].rearrange("p (h e d) -> p h e d", e=2, d=D // 2)
                nc.vector.scalar_tensor_tensor(out=dst[:, :, 0, :], in0=src[:, :, 0, :], scalar=cos, in1=sn[:, :, 1, :],
                                               op0=ALU.mult, op1=ALU.subtract)
                nc.vector.scalar_tensor_tensor(out=dst[:, :, 1, :], in0=src[:, :, 1, :], scalar=cos, in1=sn[:, :, 0, :],
                                               op0=ALU.mult, op1=ALU.add).then_inc(S["rope"], 1)

            def scores(b, h):
                dve.wait_ge(S["sc"], b * H + h + 1)
                wait(dve, "pr", b * H + max(h - R_SM + 1, 0))
                if not isinstance(b, int):
                    dve.sem_inc(S["dve_tick"], 1)
                for t in range(NT):
                    cols = slice(0, P) if t == 0 else slice(P, SW)
                    m = mask[:, P:2 * P] if t == 0 else mask
                    last = nc.vector.tensor_tensor_reduce(out=SM[:, h % R_SM, cols], in0=bS[h % R_S][:, cols], in1=m, scale=1.0,
                                                          scalar=HUGE, op0=ALU.add, op1=ALU.min, accum_out=nb[:, h, t:t + 1])
                last.then_inc(S["sm"], 1)

            def probs(b, h):
                dve.wait_ge(S["pt"], b * H + h + 1)
                wait(dve, "pv", b * NG + max((h - R_PTS) // 4 + 1, 0))
                nc.vector.tensor_copy(PTS[:, h % R_PTS, :], bPT[h % R_PT][:, 0:SW]).then_inc(S["pts"], 1)

            def normalise(n, u, bank):
                half, t = divmod(u, NT)
                dve.wait_ge(S["ob"], n * 4 + u + 1)
                src = bJ[bank][:, :].rearrange("p (h d) -> p h d", d=32)
                r = rden[:, u, :].rearrange("p (h o) -> p h o", o=1)
                nc.vector.reciprocal(r, src[:, :, D:D + 1]).then_inc(S["rd"], 1)
                wait(dve, "oT", n * 2)
                dve.wait_ge(S["rd"], n * 4 + u + 1)
                nc.vector.tensor_tensor(ON[:, t, half * (C // 2):(half + 1) * (C // 2)].rearrange("p (h d) -> p h d", d=D),
                                        src[:, :, 0:D], r.broadcast_to((P, H // 2, D)), ALU.mult).then_inc(S["on"], 1)

            def chan_lo(n, k, bank):
                dve.wait_ge(S["oh"], n * 2 + k + 1)
                nc.vector.tensor_tensor(OL[:, 2 * k:2 * k + 2, :], bJ[bank][:, :].rearrange("p (c t) -> p c t", c=2),
                                        OH[:, 2 * k:2 * k + 2, :].bitcast(F32), ALU.subtract).then_inc(S["ol"], 1)

            def residual(n, t, bank):
                dve.wait_ge(S["xn_in"], n * 16 + 16)
                dve.wait_ge(S["yp"], n * NT + t + 1)
                nc.vector.tensor_tensor(RES[:, t, :], bJ[bank][:, :], RES[:, t, :], ALU.add).then_inc(S["res"], 1)
                dve.wait_ge(S["res"], n * NT + t + 1)
                nc.vector.bn_stats(st[:, t, :], RES[:, t, :]).then_inc(S["ln_dve"], 1)
                dve.wait_ge(S["ln_dve"], n * 2 * NT + 2 * t + 1)
                if not isinstance(n, int):
                    dve.sem_inc(S["dve_tick"], 1)
                nc.vector.bn_aggr(mv[:, t, 0:2], st[:, t, :]).then_inc(S["ln_dve"], 1)
                dve.wait_ge(S["ln_dve"], n * 2 * NT + 2 * t + 2)
                nc.vector.tensor_scalar(mv[:, t, 2:3], mv[:, t, 1:2], EPS, None, ALU.add).then_inc(S["ln_var"], 1)

            def layernorm(n, t):
                dve.wait_ge(S["ln_rstd"], n * NT + t + 1)
                nc.vector.tensor_scalar(Y[:, bass.ds(n * (NT * C) + t * C, C)], RES[:, t, :], mv[:, t, 0:1], mv[:, t, 3:4],
                                        ALU.subtract, ALU.mult).then_inc(S["y_out"], 1)

            def y_lo(t, bank):
                half, r = divmod(t, NTT // NHALF)
                dve.wait_ge(S["yh"], t + 1)
                nc.vector.tensor_tensor(YL[half][:, :, r * P:(r + 1) * P], bJ[bank][:, :].rearrange("p (c t) -> p c t", c=NC),
                                        YH[half][:, :, r * P:(r + 1) * P].bitcast(F32), ALU.subtract).then_inc(S["yl"], 1)

            def shared(b, item):
                kind, n, rel, bank, _, _ = item
                if kind == "proj" and n < 4:
                    rotate(b + rel, n, bank)
                elif kind == "back":
                    normalise(b + rel, n, bank)
                elif kind == "chan":
                    chan_lo(b + rel, n, bank)
                elif kind == "outp":
                    residual(b + rel, n, bank)
                elif kind == "yt":
                    y_lo(n, bank)

            def run(b, kind):
                if kind == "before":
                    dve.wait_ge(S["k_in"], 16)
                    w_lo(0)
                    w_lo(1)
                    rotate(0, 0, 0)
                    rotate(0, 1, 1)
                    w_lo(2)
                    rotate(0, 2, 1)
                    w_lo(3)
                    rotate(0, 3, 0)
                    dve.wait_ge(S["w_lo"], 4)
                    nc.vector.memset(QS[:, :, :, :].rearrange("p a t (h k) -> p (a t h) k", k=SLOT)[:, :, KROWS:SLOT].bitcast(F32), 0.0).then_inc(S["pads"], 1)
                    return
                if kind == "after":
                    for item in PREV:
                        shared(b, item)
                    for t in range(NT):
                        layernorm(b - 1, t)
                    return
                for s in steps(kind):
                    if s < H:
                        scores(b, s)
                    if LAG_PT <= s < H + LAG_PT:
                        probs(b, s - LAG_PT)
                    for item in finished(kind, s):
                        shared(b, item)
                    if kind != "first":
                        for item in finished(kind, s - 2):
                            if item[0] == "outp":
                                layernorm(b - 1, item[1])
                for item in finished(kind, STEPS):
                    shared(b, item)

            rounds(dve, run)

            def inner(n, at, slot):
                k = [n * 5]

                def link(ins):
                    ins.then_inc(S["f_dve"], 1)
                    k[0] = k[0] + 1
                    dve.wait_ge(S["f_dve"], k[0])

                dve.wait_ge(S["sil"], n + 1)
                dve.wait_ge(S["u_mm"], n + 1)
                link(nc.vector.tensor_tensor(f_v[:, :], f_sil[:, slot, :], bU[slot][:, :], ALU.mult))
                link(nc.vector.tensor_scalar(f_c[:, 0, :], f_v[:, :], -128.0, 127.0, ALU.max, ALU.min))
                nc.vector.tensor_scalar(f_r[:, 0, :], f_c[:, 0, :], MAGIC, -MAGIC, ALU.add, ALU.add).then_inc(S["f_round"], 1)
                dve.wait_ge(S["f_round"], n + 1)
                link(nc.vector.tensor_tensor(f_d[:, 0, :], f_r[:, 0, :], f_c[:, 0, :], ALU.subtract))
                link(nc.vector.tensor_tensor(f_e[:, 0, :], f_d[:, 0, :], f_r[:, 0, :], ALU.mult))
                dve.wait_ge(S["f_sgn"], n + 1)
                link(nc.vector.scalar_tensor_tensor(out=f_d[:, 1, :], in0=f_e[:, 0, :], scalar=0.0, in1=f_s[:, 0, :], op0=ALU.is_gt, op1=ALU.mult))
                nc.vector.tensor_tensor(IQ[:, bass.ds(at, HALF)], f_r[:, 0, :], f_d[:, 1, :], ALU.subtract).then_inc(S["iq"], 1)

            for t in range(NTT // 2, NTT):
                y_lo(t, t % 2)
            inner(0, 0, 0)
            inner(1, B * T, 1)
            inner(2, HALF, 0)
            inner(3, B * T + HALF, 1)
            with dve.Fori(2, NI - 1, 2) as i:
                for u in range(2):
                    for half in range(NHALF):
                        inner(NHALF * (i + u) + half, (i + u) * (B * T) + half * HALF, half)
            for half in range(NHALF):
                inner(NHALF * (NI - 1) + half, (NI - 1) * (B * T) + half * HALF, half)

            def clip(t):
                r = t % 2
                dve.wait_ge(S["d_sb"], t + 1)
                nc.vector.tensor_scalar(f_c[:, r, :], f_sil[:, r, :], -128.0, 127.0, ALU.max, ALU.min).then_inc(S["o_clip"], 1)
                dve.wait_ge(S["o_clip"], t + 1)
                nc.vector.tensor_scalar(f_r[:, r, :], f_c[:, r, :], MAGIC, -MAGIC, ALU.add, ALU.add).then_inc(S["o_round"], 1)

            def second_residual(t):
                r = t % 2
                k = [t * 5]

                def link(ins):
                    ins.then_inc(S["o_dve"], 1)
                    k[0] += 1
                    dve.wait_ge(S["o_dve"], k[0])

                dve.wait_ge(S["o_sgn"], t + 1)
                dve.wait_ge(S["o_pool"], 2 * t + 2)
                link(nc.vector.scalar_tensor_tensor(out=f_v[:, :], in0=f_e[:, r, :], scalar=0.0, in1=f_s[:, r, :], op0=ALU.is_gt, op1=ALU.mult))
                link(nc.vector.tensor_tensor(z[:, r, :], f_r[:, r, :], f_v[:, :], ALU.subtract))
                link(nc.vector.tensor_tensor(z[:, r, :], z[:, r, :], Y[:, t * C:(t + 1) * C], ALU.add))
                link(nc.vector.bn_stats(sz[:, r, :], z[:, r, :]))
                link(nc.vector.bn_aggr(mz[:, r, 0:2], sz[:, r, :]))
                nc.vector.tensor_scalar(mz[:, r, 2:3], mz[:, r, 1:2], EPS, None, ALU.add).then_inc(S["z_var"], 1)

            def second_layernorm(t):
                r = t % 2
                dve.wait_ge(S["z_rstd"], t + 1)
                if t >= 2:
                    dve.wait_ge(S[f"stored{r}"], 16 * (t // 2))
                nc.vector.tensor_scalar(o[:, r, :], z[:, r, :], mz[:, r, 0:1], mz[:, r, 3:4], ALU.subtract, ALU.mult).then_inc(S["z_out"], 1)

            for t in range(NTT + 1):
                if t < NTT:
                    clip(t)
                if t >= 1:
                    second_residual(t - 1)
                    if t < NTT:
                        second_layernorm(t - 1)
            second_layernorm(NTT - 1)

        @block.tensor
        def _(pe):
            def product(dst, c, ah, al, bh, bl):
                nc.tensor.matmul(dst, ah, bh, start=(c == 0), stop=False)
                nc.tensor.matmul(dst, ah, bl, start=False, stop=False)
                return nc.tensor.matmul(dst, al, bh, start=False, stop=(c == NC - 1))

            def wait_read(b, kind, item):
                mine = [i for i in SHARED[kind] if i[3] == item[3]]
                at = mine.index(item)
                if at:
                    name, n, rel = mine[at - 1][:3]
                elif kind == "before":
                    return
                else:
                    name, n, rel = [i for i in SHARED[BEFORE[kind]] if i[3] == item[3]][-1][:3]
                    rel -= 1
                sem, per, count = {"back": ("on", 4, n + 1), "chan": ("ol", 2, n + 1), "outp": ("res", NT, n + 1), "yt": ("yl", 0, n + 1),
                                   "proj": ("rope", 4, n + 1) if n < 4 else ("v_sb", 2, n - 3)}[name]
                wait(pe, sem, (b + rel) * per + count)

            def shared(b, kind, item, c):
                what, n, rel, bank, _, _ = item
                m = b + rel
                dst = bJ[bank]
                if c == 0:
                    wait_read(b, kind, item)
                if what == "proj":
                    w, t = divmod(n, NT)
                    if c == 0:
                        pe.wait_ge(S["xh"], m + 1)
                        pe.wait_ge(S["xl"], m + 1)
                        pe.wait_ge(S["w_lo"], w + 1)
                    tok = slice(t * P, (t + 1) * P)
                    last = product(dst[:, :], c, XH[:, c, tok], XL[:, c, tok], WQH[:, w, c, :], WQL[:, w, c, :])
                    done = "proj"
                elif what == "back":
                    half, t = divmod(n, NT)
                    pe.wait_ge(S["ot"], m * NG + (half + 1) * (NG // 2))
                    for g in range(NG // 2):
                        last = nc.tensor.transpose(dst[:, g * P:(g + 1) * P], OT[:, half * (NG // 2) + g, t * P:(t + 1) * P], ident)
                    done = "ob"
                elif what == "chan":
                    pe.wait_ge(S["on"], m * 4 + 2 * (n + 1))
                    for i in range(2):
                        for t in range(NT):
                            last = nc.tensor.transpose(dst[:, i * T + t * P:i * T + (t + 1) * P],
                                                       ON[:, t, (2 * n + i) * P:(2 * n + i + 1) * P], ident)
                    done = "oT"
                elif what == "outp":
                    if c == 0:
                        pe.wait_ge(S["ol"], m * 2 + 2)
                    tok = slice(n * P, (n + 1) * P)
                    last = product(dst[:, :], c, OH[:, c, tok], OL[:, c, tok], WOH[:, c, :], WOL[:, c, :])
                    done = "yp"
                else:
                    pe.wait_ge(S["y_out"], n + 1)
                    for i in range(NC):
                        last = nc.tensor.transpose(dst[:, i * P:(i + 1) * P], Y[:, n * C + i * P:n * C + (i + 1) * P], ident)
                    done = "yt"
                if c == item[5] - 1:
                    last.then_inc(S[done], 1)

            def stack_t(b, j):
                if j == 0:
                    pe.wait_ge(S["lo"], b * 4 + 4)
                wait(pe, "qkt", b * NBLK + j)
                for a in range(2):
                    for t in range(NT):
                        last = nc.tensor.transpose(bTR[:, a * T + t * P:a * T + (t + 1) * P].bitcast(F32R),
                                                   QS[:, a, t, j * P:(j + 1) * P], identr[:, :])
                last.then_inc(S["tr"], 1)

            def scores(b, h):
                j, half = divmod(h, 2)
                rows = slice(half * SLOT, half * SLOT + KROWS)
                pe.wait_ge(S["qkt"], b * NBLK + j + 1)
                wait(pe, "sm", b * H + max(h - R_S + 1, 0))
                q = QKT[rows, j % R_QKT, 0, :]
                k = QKT[rows, j % R_QKT, 1, :]
                nc.tensor.matmul(bS[h % R_S][:, 0:P], q[:, 0:P], k[:, 0:P], start=True, stop=True)
                nc.tensor.matmul(bS[h % R_S][:, P:SW], q[:, P:T], k[:, 0:T], start=True, stop=True).then_inc(S["sc"], 1)

            def probs_t(b, h):
                pe.wait_ge(S["pr"], b * H + h + 1)
                wait(pe, "pts", b * H + max(h - R_PT + 1, 0))
                for i in range(3):
                    last = nc.tensor.transpose(bPT[h % R_PT][:, i * P:(i + 1) * P], PR[:, h % R_P, i * P:(i + 1) * P], ident)
                last.then_inc(S["pt"], 1)

            def pv(b, g):
                wait(pe, "ot", b * NG + g)
                pe.wait_ge(S["pts"], b * H + 4 * (g + 1))
                if g == 0:
                    pe.wait_ge(S["v_sb"], b * 2 + 2)
                for key, to, cols in ((0, slice(0, T), slice(0, T)), (1, slice(P, T), slice(T, SW))):
                    for r in range(4):
                        h = 4 * g + r
                        last = nc.tensor.matmul(bAV[32 * r:32 * r + 32, to], V[:, key, h, :], PTS[:, h % R_PTS, cols],
                                                start=(key == 0), stop=(key == 1))
                last.then_inc(S["pv"], 1)

            def up(n, i, slot, half, bank):
                pe.wait_ge(S["gu_lo"], i + 1)
                for k, (dst, done, read) in enumerate(((bG, "g_mm", "sil"), (bU, "u_mm", "f_round"))):
                    wait(pe, read, n - 1)
                    wh, wl = (m[:, slot, :].rearrange("p (k c n) -> p k c n", k=2, c=NC) for m in (GH, GL))
                    for c in range(NC):
                        last = product(dst[bank][:, :], c, wh[:, k, c, :], wl[:, k, c, :], YH[half][:, c, :], YL[half][:, c, :])
                    last.then_inc(S[done], 1)

            def run(b, kind):
                if kind == "before":
                    for item in NEXT:
                        for c in range(NC):
                            shared(b, kind, item, c)
                    return
                if kind == "after":
                    for item in PREV:
                        for c in range(item[5]):
                            shared(b, kind, item, c)
                        if item[0:2] == ("back", 3):
                            pe.wait_ge(S["pts"], B * H)
                            pe.wait_ge(S["yl"], NTT // 2)
                            up(0, 0, 0, 0, 0)
                    up(1, 1, 1, 0, 1)
                    return
                if kind == "first":
                    pe.wait_ge(S["pads"], 1)
                    pe.wait_ge(S["identr"], 1)
                stack_t(b, 0)
                stack_t(b, 1)
                for s in steps(kind):
                    if s % 2 == 0 and s // 2 + 2 < NBLK:
                        stack_t(b, s // 2 + 2)
                    if s < H:
                        scores(b, s)
                    if LAG_PT <= s < H + LAG_PT:
                        probs_t(b, s - LAG_PT)
                    if s >= LAG_AV and (s - LAG_AV) % 4 == 3:
                        pv(b, (s - LAG_AV) // 4)
                    for item in SHARED[kind]:
                        if item[4] <= s < item[4] + item[5]:
                            shared(b, kind, item, s - item[4])

            pe.wait_ge(S["k_in"], 16)
            rounds(pe, run)

            pe.wait_ge(S["res"], NTT)
            for t in range(NTT // 2, NTT):
                pe.wait_ge(S["y_out"], t + 1)
                wait(pe, "yl", t - 1)
                for c in range(NC):
                    last = nc.tensor.transpose(bJ[t % 2][:, c * P:(c + 1) * P], Y[:, t * C + c * P:t * C + (c + 1) * P], ident)
                last.then_inc(S["yt"], 1)
            pe.wait_ge(S["yl"], NTT)
            up(2, 0, 0, 1, 0)
            up(3, 1, 1, 1, 1)
            with pe.Fori(2, NI - 1, 2) as i:
                for u in range(2):
                    for half in range(NHALF):
                        up(NHALF * (i + u) + half, i + u, u, half, half)
            for half in range(NHALF):
                up(NHALF * (NI - 1) + half, NI - 1, 0, half, half)
            pe.wait_ge(S["wd_lo"], NI)
            for t in range(NTT):
                wait(pe, "d_sb", t - 1)
                for i in range(NI):
                    if t == 0 and i == NI - 1:
                        pe.wait_ge(S["iq"], NHALF * NI)
                    elif t == 0 and i == 0:
                        pe.wait_ge(S["iq"], NHALF * (NI - 1))
                    a = IQ[:, i * B * T + t * P:i * B * T + (t + 1) * P]
                    nc.tensor.matmul(bD[t % 2][:, :], a, DH[:, i, :], start=(i == 0), stop=False)
                    last = nc.tensor.matmul(bD[t % 2][:, :], a, DL[:, i, :], start=False, stop=(i == NI - 1))
                last.then_inc(S["dn"], 1)


def kernel(**inputs):
    import numpy as np
    import concourse.bacc as bacc
    from concourse.bass_utils import run_bass_kernel_spmd

    def pairs_apart(w):
        return w.reshape(H, D // 2, 2, C).transpose(0, 2, 1, 3).reshape(C, C)

    def padded(w):
        return np.concatenate([w, np.zeros((NI * P - INTER, C), w.dtype)])

    a = {k: np.asarray(v) for k, v in inputs.items()}
    xs = a["L0_attn_x"]
    wqkvo = np.stack([pairs_apart(a["L0_attn_wq"]).T, pairs_apart(a["L0_attn_wk"]).T, a["L0_attn_wv"].T, a["L0_attn_wo"].T])
    gu = np.stack([padded(a["L0_ffn_w_gate"]), padded(a["L0_ffn_w_up"])])
    gu = gu.reshape(2, NI, P, NC, P).transpose(1, 4, 0, 3, 2).reshape(NI, P, 2 * NC * P)
    wd = padded(a["L0_ffn_w_down"].T).reshape(NI, P, C)

    k = np.zeros((P, NK), np.float32)
    k[:, K_ID:K_ID + P] = np.eye(P)
    k[:, K_MASK + P:K_MASK + 2 * P] = np.triu(np.full((P, P), BIG), 1)
    theta = np.arange(T, dtype=np.float32).reshape(NT, P)
    for t in range(NT):
        for j, v in enumerate((-D ** -0.5 * np.cos(theta[t]), -D ** -0.5 * np.sin(theta[t]), np.cos(theta[t]), np.sin(theta[t]))):
            k[:, K_ROT + 4 * t + j] = v
    k[:, K_HALF] = -0.5

    nc = bacc.Bacc("TRN2", target_bir_lowering=False, num_devices=1)
    arrays, args = {}, []
    for name, v in (("xT", xs.transpose(0, 2, 1)), ("x", xs), ("wqkvo", wqkvo), ("wgu", gu), ("wd", wd), ("consts", k)):
        v = np.ascontiguousarray(v)
        arrays[name] = v
        args.append(nc.dram_tensor(name, v.shape, mybir.dt.from_np(v.dtype), kind="ExternalInput").ap())
    args.append(nc.dram_tensor("out", (B * T, C), F32, kind="ExternalOutput").ap())
    layer(nc, *args)
    r = run_bass_kernel_spmd(nc, [arrays], core_ids=[0])
    return r.results[0]["out"].reshape(B, T, C)
```

```python
import concourse.bass as bass
from concourse import mybir
from contextlib import ExitStack

F32 = mybir.dt.float32
F32R = mybir.dt.float32r
ALU = mybir.AluOpType
ACT = mybir.ActivationFunctionType

P = 128
B, T, C, H, D = 4, 256, 512, 32, 16
INTER = 1376
NI = -(-INTER // P)
NT = T // P
NTT = B * NT
NC = C // P
NBLK = H // 2
NG = H // 4
SLOT = 64
KROWS = 3 * D
SW = 3 * P
BIG = 1.0e30
HUGE = 3.0e38
MAGIC = 1.5 * 2.0 ** 23
EPS = 1e-5
HALF = 512
NHALF = B * T // HALF

K_ID = 0
K_MASK = K_ID + P
K_ROT = K_MASK + 2 * P
K_HALF = K_ROT + 4 * NT
NK = K_HALF + 1

R_S, R_PT, R_QKT, R_SM, R_P, R_PTS = 2, 2, 4, 2, 4, 8
LAG_PT, LAG_AV = 3, 5
STACKS_AHEAD = 3

VALUES = [("proj", 4, 0, 0, 0, 2), ("proj", 5, 0, 1, 2, 2)]
BACK = [("back", 0, -1, 0, 6, 1), ("back", 1, -1, 1, 7, 1), ("back", 2, -1, 0, 8, 1), ("back", 3, -1, 1, 9, 1),
        ("chan", 0, -1, 0, 10, 1), ("chan", 1, -1, 1, 11, 1)]
OUTP = [("outp", 0, -1, 0, 25, 3), ("outp", 1, -1, 1, 28, 3)]
NEXT = [("proj", 0, 1, 0, 14, 2), ("proj", 1, 1, 1, 16, 3), ("proj", 2, 1, 0, 20, 2), ("proj", 3, 1, 1, 22, 2)]
NEXT1 = [("proj", 0, 1, 0, 6, 5), ("proj", 1, 1, 1, 11, 4), ("proj", 2, 1, 0, 15, 4), ("proj", 3, 1, 1, 19, 5)]
LAST = [("yt", 0, 0, 0, 13, 1), ("yt", 1, 0, 1, 14, 1), ("yt", 2, 0, 0, 16, 1), ("yt", 3, 0, 1, 18, 1),
        ("outp", 0, -1, 0, 19, 2), ("outp", 1, -1, 1, 20, 2),
        ("gate", 0, 0, 0, 22, 3), ("up", 0, 0, 1, 24, 3), ("gate", 1, 0, 0, 28, 2), ("up", 1, 0, 1, 29, 2)]
AFTER = [("yt", 4, 0, 0, 0, 1), ("yt", 5, 0, 1, 2, 1)] + BACK + OUTP + [("yt", 6, 0, 0, 0, 0), ("yt", 7, 0, 1, 0, 0)]


def chunks(item):
    return NC if item[0] in ("proj", "outp", "gate", "up") else 1


def by_step(items):
    return sorted(items, key=lambda x: x[4])


SHARED = {
    "before": [("proj", m, 1, m, 0, 0) for m in range(4)],
    "first": by_step(VALUES + NEXT1),
    "middle": by_step(VALUES + BACK + NEXT + OUTP),
    "last": by_step(VALUES + BACK + LAST),
    "after": AFTER,
}
BEFORE = {"first": "before", "middle": "middle", "last": "middle", "after": "last"}
XH_STEP = {"first": 3, "middle": 7}
HI_STEP = {18: (0, 0), 23: (1, 0), 24: (2, 0), 26: (3, 0), 27: (0, 1), 29: (1, 1), 30: (2, 1), 31: (3, 1)}
GU_STEP = {6: 0, 7: 1, 19: 2, 26: 3}


def layer(nc, xT, x, wqkvo, wgu, wd, consts, out):
    ctx = ExitStack()
    with ctx:
        def sb(name, shape, dt, where=ctx):
            return where.enter_context(nc.sbuf_tensor(name, shape, dt))

        K = sb("K", [P, NK], F32)
        ident = K[:, K_ID:K_ID + P]
        mask = K[:, K_MASK:K_MASK + 2 * P]
        Y = sb("Y", [P, NTT * C], F32)
        gu_raw = sb("gu_raw", [P, 2, 2 * NC * P], F32)
        wd_raw = sb("wd_raw", [P, 2, C], F32)

        mz = sb("mz", [P, 2, 8], F32)
        sz = sb("sz", [P, 2, 6], F32)
        identr = sb("identr", [P, P], F32R)

        ph1 = ctx.enter_context(ExitStack())
        WQH = sb("WQH", [P, 3, NC, C], F32R, ph1)
        WQL = sb("WQL", [P, 3, NC, C], F32R, ph1)
        XH = sb("XH", [P, NC, T], F32R, ph1)
        with ExitStack() as phx:
            XR = sb("XR", [P, NC, T], F32, phx)
        XL = sb("XL", [P, NC, T], F32R, ph1)
        T1 = sb("T1", [P, C], F32, ph1)
        RQ = sb("RQ", [P, 4, C], F32, ph1)
        QS = sb("QS", [P, 2, NT, NBLK * P], F32R, ph1)
        QKT = sb("QKT", [P, R_QKT, 2, T], F32R, ph1)
        SM = sb("SM", [P, R_SM, SW], F32, ph1)
        PR = sb("PR", [P, R_P, SW], F32, ph1)
        with ExitStack() as ph0:
            w_raw = sb("w_raw", [P, 4, NC, C], F32, ph0)
        PTS = sb("PTS", [P, R_PTS, SW], F32, ph1)
        OT = sb("OT", [P, NG, T], F32, ph1)
        ON = sb("ON", [P, NT, C], F32, ph1)
        OH = sb("OH", [P, NC, T], F32R, ph1)
        OL = sb("OL", [P, NC, T], F32R, ph1)
        V = sb("V", [P, NT, H, 32], F32, ph1)
        WOH = sb("WOH", [P, NC, C], F32R, ph1)
        WOL = sb("WOL", [P, NC, C], F32R, ph1)
        RES = sb("RES", [P, NT, C], F32, ph1)
        nb = sb("nb", [P, H, NT], F32, ph1)
        rden = sb("rden", [P, 4, H // 2], F32, ph1)
        mv = sb("mv", [P, NT, 8], F32, ph1)
        st = sb("st", [P, NT, 6], F32, ph1)
        ph1.close()

        with ExitStack() as ph3:
            d_sb = sb("d_sb", [P, 2, C], F32, ph3)
            d_c = sb("d_c", [P, 2, C], F32, ph3)
            d_r = sb("d_r", [P, 2, C], F32, ph3)
            d_s = sb("d_s", [P, 2, C], F32, ph3)
            d_d = sb("d_d", [P, 2, C], F32, ph3)
            d_e = sb("d_e", [P, 2, C], F32, ph3)
            z = sb("z", [P, 2, C], F32, ph3)
            o = sb("o", [P, 2, C], F32, ph3)
        NS = 4
        GH = sb("GH", [P, NS, 2 * NC * P], F32R)
        GL = sb("GL", [P, NS, 2 * NC * P], F32R)
        YH = [sb("YH0", [P, NC, HALF], F32R)]
        YL = [sb("YL0", [P, NC, HALF], F32R)]
        YH.append(sb("YH1", [P, NC, HALF], F32R))
        YL.append(sb("YL1", [P, NC, HALF], F32R))
        f_sil = sb("f_sil", [P, 2, HALF], F32)
        f_v = sb("f_v", [P, 4, HALF], F32)
        f_c = sb("f_c", [P, HALF], F32)
        f_r = sb("f_r", [P, HALF], F32)
        f_d = sb("f_d", [P, 2, HALF], F32)
        f_s = sb("f_s", [P, HALF], F32)
        f_e = sb("f_e", [P, HALF], F32)
        IQ = sb("IQ", [P, NI * B * T], F32R)
        DH = sb("DH", [P, NI, C], F32R)
        DL = sb("DL", [P, NI, C], F32R)

        bank = [ctx.enter_context(nc.psum_tensor(f"bank{i}", [P, 512], F32)) for i in range(8)]
        bJ, bAV, bTR, bS, bPT = bank[0:2], bank[2], bank[3], bank[4:6], bank[6:8]
        shared_bank = bJ + bS
        bD, bG, bU = bank[2:4], bank[4:6], bank[6:8]

        names = """w_in0 w_in1 w_in2 w_in3 w_in4 w_in5 w_in6 w_in7 k_in xt_in xn_in gu_in0 gu_in1 wd_in0 wd_in1
                   identr pads v_init w_hi w_lo v_lo xh xl
                   proj t1 rope hi lo v_sb tr qkt sc sm pr pt pts pv ot ob rd on oT oh ol yp
                   res ln_dve ln_var ln_rstd y_out yt yh yl dve_tick
                   gu_hi gu_lo wd_hi wd_lo g_mm u_mm gu_out sil uv f_dve f_round f_sgn iq
                   dn d_out o_clip o_round o_sgn o_pool o_dve z_var z_rstd z_out stored0 stored1""".split()
        S = {n: ctx.enter_context(nc.semaphore("s_" + n)) for n in names}
        block = ctx.enter_context(nc.Block())


        def wait(eng, name, value):
            if not (isinstance(value, int) and value <= 0):
                eng.wait_ge(S[name], value)

        def rounds(eng, run):
            run(-1, "before")
            run(0, "first")
            with eng.Fori(1, B - 1) as b:
                run(b, "middle")
            run(B - 1, "last")
            run(B, "after")

        def steps(kind):
            return range({"before": 0, "after": LAG_AV}.get(kind, H))

        def trailing(b, kind, s, lag):
            if s < lag:
                return [(b - 1, s - lag + H)] if kind in ("middle", "last", "after") else []
            return [(b, s - lag)] if kind != "after" else []

        def leading(b, kind, s):
            if (s + STACKS_AHEAD) % 2 or kind == "after":
                return []
            j = (s + STACKS_AHEAD) // 2
            if j < NBLK:
                return [(b, j)]
            return [(b + 1, j - NBLK)] if kind != "last" else []

        def finished(kind, s):
            return [i for i in SHARED[kind] if (LAG_AV - 1 + VALUES.index(i) if i in VALUES else i[4] + i[5]) == s]

        def finished_dve(kind, s):
            return [i for i in SHARED[kind] if i[4] + i[5] + (i[0] in ("proj", "chan", "yt")) == s]


        @block.sync
        def _(sp):
            def load_xt(b):
                wait(sp, "proj", b * 6)
                sp.dma_start(XR[:, :, :], xT[bass.ds(b, 1)].rearrange("o (c p) t -> p (o c) t", p=P)).then_inc(S["xt_in"], 16)

            def load_xn(b):
                wait(sp, "y_out", b * NT)
                sp.dma_start(RES[:, :, :], x[bass.ds(b, 1)].rearrange("o (t p) c -> p (o t) c", p=P)).then_inc(S["xn_in"], 16)

            load_xt(0)
            for u in range(8):
                w, c = divmod(u * 2, NC)
                sp.dma_start(w_raw[:, w, c:c + 2, :], wqkvo[w, c * P:(c + 2) * P].rearrange("(c p) n -> p c n", p=P)).then_inc(S[f"w_in{u}"], 16)
                if u == 1:
                    sp.dma_start(K[:, :], consts).then_inc(S["k_in"], 16)
            load_xt(1)
            load_xn(0)
            with sp.Fori(2, B) as b:
                load_xt(b)
                load_xn(b - 1)

            def load_gu(i, slot):
                wait(sp, "gu_lo", i - 1)
                sp.dma_start(gu_raw[:, slot, :], wgu[bass.ds(i, 1)].rearrange("o p n -> p (o n)")).then_inc(S[f"gu_in{slot}"], 16)

            def load_wd(i, slot):
                wait(sp, "wd_lo", i - 1)
                sp.dma_start(wd_raw[:, slot, :], wd[bass.ds(i, 1)].rearrange("o p n -> p (o n)")).then_inc(S[f"wd_in{slot}"], 16)

            load_gu(0, 0)
            load_wd(0, 0)
            load_gu(1, 1)
            load_wd(1, 1)
            load_gu(2, 0)
            load_gu(3, 1)
            load_xn(B - 1)
            load_gu(4, 0)
            load_gu(5, 1)
            load_wd(2, 0)
            load_wd(3, 1)
            with sp.Fori(NS + 2, NI - 1, 2) as i:
                for u in range(2):
                    load_gu(i + u, u)
                    load_wd(i + u - 2, u)
            load_gu(NI - 1, 0)
            for i in range(NI - 3, NI):
                load_wd(i, i % 2)
            for t in range(NTT):
                sp.wait_ge(S["z_out"], t + 1)
                sp.dma_start(out[t * P:(t + 1) * P, :], o[:, t % 2, :]).then_inc(S[f"stored{t % 2}"], 16)
            for r in range(2):
                sp.wait_ge(S[f"stored{r}"], 16 * NTT // 2)

        @block.gpsimd
        def _(pool):
            nc.gpsimd.memset(V[:, :, :, :], 0.0).then_inc(S["v_init"], 1)
            pool.wait_ge(S["v_init"], 1)
            nc.gpsimd.memset(V[:, :, :, D:D + 1], 1.0).then_inc(S["v_init"], 1)

            def split_gu(i, raw, slot):
                pool.wait_ge(S["gu_hi"], i + 1)
                nc.gpsimd.tensor_tensor(GL[:, slot, :], gu_raw[:, raw, :], GH[:, slot, :].bitcast(F32), ALU.subtract).then_inc(S["gu_lo"], 1)

            def split_wd(i, slot):
                pool.wait_ge(S["wd_hi"], i + 1)
                at = bass.ds(i, 1)
                nc.gpsimd.tensor_tensor(DL[:, at, :].rearrange("p o n -> p (o n)"), wd_raw[:, slot, :],
                                        DH[:, at, :].rearrange("p o n -> p (o n)").bitcast(F32), ALU.subtract).then_inc(S["wd_lo"], 1)

            def run(b, kind):
                def rstd(t):
                    pool.wait_ge(S["ln_var"], (b - 1) * NT + t + 1)
                    nc.gpsimd.tensor_tensor(mv[:, t, 3:4], mv[:, t, 2:3], K[:, K_HALF:K_HALF + 1], ALU.pow).then_inc(S["ln_rstd"], 1)

                if kind == "last":
                    split_gu(0, 0, 0)
                    split_gu(1, 1, 1)
                    split_gu(2, 0, 2)
                    rstd(0)
                    rstd(1)
                    split_gu(3, 1, 3)
                    return
                if kind == "after":
                    rstd(0)
                    rstd(1)
                    return
                n = b + 1
                if kind == "before":
                    for u in (4, 5):
                        pool.wait_ge(S["w_hi"], u + 1)
                        c = slice(u % 2 * 2, u % 2 * 2 + 2)
                        nc.gpsimd.tensor_tensor(WQL[:, 2, c, :], w_raw[:, 2, c, :], WQH[:, 2, c, :].bitcast(F32), ALU.subtract).then_inc(S["v_lo"], 1)
                else:
                    pool.wait_ge(S["xh"], n + 1)
                    nc.gpsimd.tensor_tensor(XL[:, :, :], XR[:, :, :], XH[:, :, :].bitcast(F32), ALU.subtract).then_inc(S["xl"], 1)
                for half in range(2):
                    for m in range(4):
                        a, t = divmod(m, NT)
                        pool.wait_ge(S["hi"], n * 8 + half * 4 + m + 1)
                        heads = slice(half * (H // 2), (half + 1) * (H // 2))
                        q = RQ[:, m, :].rearrange("p (h d) -> p h d", d=D)[:, heads, :]
                        s = QS[:, a, t, :].rearrange("p (h k d) -> p h k d", k=4, d=D)[:, heads, :, :]
                        nc.gpsimd.tensor_tensor(s[:, :, 2 - a, :], q, s[:, :, 0, :].bitcast(F32), ALU.subtract).then_inc(S["lo"], 1)
                    if kind == "middle":
                        rstd(half)

            rounds(pool, run)

            split_wd(0, 0)
            split_wd(1, 1)
            split_gu(4, 0, 0)
            split_wd(2, 0)
            split_gu(5, 1, 1)
            split_wd(3, 1)
            with pool.Fori(NS, NI - 3, 2) as i:
                for u in range(2):
                    split_gu(i + u + 2, u, u)
                    split_wd(i + u, u)
            split_gu(NI - 1, 0, 0)
            for i in range(NI - 3, NI):
                split_wd(i, i % 2)

            def rest(t):
                r = t % 2
                pool.wait_ge(S["o_round"], t + 1)
                nc.gpsimd.tensor_tensor(d_d[:, r, :], d_r[:, r, :], d_c[:, r, :], ALU.subtract).then_inc(S["o_pool"], 1)
                pool.wait_ge(S["o_pool"], 2 * t + 1)
                nc.gpsimd.tensor_tensor(d_e[:, r, :], d_d[:, r, :], d_r[:, r, :], ALU.mult).then_inc(S["o_pool"], 1)

            rest(0)
            for t in range(NTT):
                if t + 1 < NTT:
                    rest(t + 1)
                pool.wait_ge(S["z_var"], t + 1)
                nc.gpsimd.tensor_tensor(mz[:, t % 2, 3:4], mz[:, t % 2, 2:3], K[:, K_HALF:K_HALF + 1], ALU.pow).then_inc(S["z_rstd"], 1)

        @block.scalar
        def _(act):
            def w_hi(u):
                w, c = divmod(u * 2, NC)
                act.wait_ge(S[f"w_in{u}"], 16)
                nc.scalar.activation(WQH[:, w, c:c + 2, :] if w < 3 else WOH[:, c:c + 2, :], w_raw[:, w, c:c + 2, :], ACT.Copy).then_inc(S["w_hi"], 1)

            def x_hi(n):
                act.wait_ge(S["xt_in"], n * 16 + 16)
                wait(act, "proj", n * 6)
                nc.scalar.activation(XH[:, :, :], XR[:, :, :], ACT.Copy).then_inc(S["xh"], 1)

            def sine(n, m, bank):
                a, t = divmod(m, NT)
                act.wait_ge(S["proj"], n * 6 + m + 1)
                wait(act, "rope", n * 4 + m)
                sin = K[:, K_ROT + 4 * t + 2 * a + 1:K_ROT + 4 * t + 2 * a + 2]
                nc.scalar.activation(T1[:, :], shared_bank[bank][:, :], ACT.Copy, scale=sin).then_inc(S["t1"], 1)

            def values(n, t, bank):
                act.wait_ge(S["proj"], n * 6 + 4 + t + 1)
                wait(act, "pv", n * NG)
                act.wait_ge(S["v_init"], 2)
                nc.scalar.activation(V[:, t, :, 0:D], shared_bank[bank][:, :].rearrange("p (h d) -> p h d", d=D), ACT.Copy).then_inc(S["v_sb"], 1)

            def high(n, m, half):
                a, t = divmod(m, NT)
                act.wait_ge(S["rope"], n * 4 + m + 1)
                wait(act, "tr", n * NBLK - (1 - half) * (NBLK // 2))
                heads = slice(half * (H // 2), (half + 1) * (H // 2))
                q = RQ[:, m, :].rearrange("p (h o d) -> p h o d", o=1, d=D)[:, heads, :, :].broadcast_to((P, H // 2, 2, D))
                s = QS[:, a, t, :].rearrange("p (h k d) -> p h k d", k=4, d=D)[:, heads, :, :]
                s = s[:, :, 0:2, :] if a == 0 else s[:, :, 0:3:2, :]
                nc.scalar.activation(s, q, ACT.Copy).then_inc(S["hi"], 1)

            def qkt(b, j):
                act.wait_ge(S["tr"], b * NBLK + j + 1)
                wait(act, "sc", b * H + 2 * (j - R_QKT + 1))
                nc.scalar.activation(QKT[:, j % R_QKT, :, :], bTR[:, :].rearrange("p (a t) -> p a t", a=2), ACT.Copy).then_inc(S["qkt"], 1)

            def exps(b, h):
                act.wait_ge(S["sm"], b * H + h + 1)
                wait(act, "pt", b * H + h - R_P + 1)
                for t in range(NT):
                    cols = slice(0, P) if t == 0 else slice(P, SW)
                    last = nc.scalar.activation(PR[:, h % R_P, cols], SM[:, h % R_SM, cols], ACT.Exp, bias=nb[:, h, t:t + 1], scale=-1.0)
                last.then_inc(S["pr"], 1)

            def pv_out(b, g):
                act.wait_ge(S["pv"], b * NG + g + 1)
                wait(act, "ob", b * 4 - (NT if g < NG // 2 else 0))
                nc.scalar.activation(OT[:, g, :], bAV[:, 0:T], ACT.Copy).then_inc(S["ot"], 1)

            def chan_hi(n, k, bank):
                act.wait_ge(S["oT"], n * 2 + k + 1)
                wait(act, "yp", n * NT)
                nc.scalar.activation(OH[:, 2 * k:2 * k + 2, :], shared_bank[bank][:, :].rearrange("p (c t) -> p c t", c=2), ACT.Copy).then_inc(S["oh"], 1)

            def y_hi(t, bank):
                half, r = divmod(t, NTT // NHALF)
                act.wait_ge(S["yt"], t + 1)
                nc.scalar.activation(YH[half][:, :, r * P:(r + 1) * P], shared_bank[bank][:, :].rearrange("p (c t) -> p c t", c=NC), ACT.Copy).then_inc(S["yh"], 1)

            def shared(b, item):
                kind, n, rel, bank, _, _ = item
                if kind == "proj" and n < 4:
                    sine(b + rel, n, bank)
                elif kind == "proj":
                    values(b + rel, n - 4, bank)
                elif kind == "chan":
                    chan_hi(b + rel, n, bank)
                elif kind == "yt":
                    y_hi(n, bank)
                elif kind == "gate":
                    act.wait_ge(S["g_mm"], n + 1)
                    nc.scalar.activation(f_sil[:, n, :], shared_bank[bank][:, :], ACT.Copy).then_inc(S["gu_out"], 1)
                elif kind == "up":
                    act.wait_ge(S["u_mm"], n + 1)
                    act.wait_ge(S["tr"], B * NBLK)
                    nc.scalar.activation(f_v[:, n, :], shared_bank[bank][:, :], ACT.Copy).then_inc(S["gu_out"], 1)

            def split_gu(i, raw, slot, used):
                act.wait_ge(S[f"gu_in{raw}"], (i - raw) * 8 + 16)
                wait(act, "u_mm", used)
                nc.scalar.activation(GH[:, slot, :], gu_raw[:, raw, :], ACT.Copy).then_inc(S["gu_hi"], 1)

            def split_wd(i, slot):
                act.wait_ge(S[f"wd_in{slot}"], (i - slot) * 8 + 16)
                nc.scalar.activation(DH[:, bass.ds(i, 1), :].rearrange("p o n -> p (o n)"), wd_raw[:, slot, :], ACT.Copy).then_inc(S["wd_hi"], 1)

            def run(b, kind):
                if kind == "before":
                    x_hi(0)
                    w_hi(0)
                    w_hi(1)
                    act.wait_ge(S["k_in"], 16)
                    nc.scalar.activation(identr[:, :], ident, ACT.Copy).then_inc(S["identr"], 1)
                    w_hi(2)
                    w_hi(3)
                    for m in range(4):
                        sine(0, m, m)
                        w_hi(4 + m)
                        high(0, m, 0)
                    high(0, 0, 1)
                    high(0, 1, 1)
                    qkt(0, 0)
                    qkt(0, 1)
                    high(0, 2, 1)
                    high(0, 3, 1)
                    return
                for s in steps(kind):
                    for n, j in leading(b, kind, s):
                        qkt(n, j)
                    if kind != "after":
                        exps(b, s)
                    for n, h in trailing(b, kind, s, LAG_AV):
                        if h % 4 == 3:
                            pv_out(n, h // 4)
                    if kind == "after":
                        for item in AFTER[:2]:
                            if s == item[4] + 1:
                                shared(b, item)
                        continue
                    for item in finished(kind, s):
                        shared(b, item)
                    if kind != "last":
                        if s == XH_STEP[kind]:
                            x_hi(b + 1)
                        if s in HI_STEP:
                            high(b + 1, *HI_STEP[s])
                    elif s in GU_STEP:
                        i = GU_STEP[s]
                        split_gu(i, i % 2, i, 0)
                if kind != "after":
                    for item in finished(kind, H):
                        shared(b, item)

            rounds(act, run)

            def silu(n, slot):
                src = f_sil[:, slot, :] if isinstance(n, int) and n < 2 else bG[slot][:, :]
                act.wait_ge(S["g_mm"], n + 1)
                if isinstance(n, int) and n < 2:
                    act.wait_ge(S["gu_out"], 2 * n + 1)
                elif isinstance(n, int) and n < 4:
                    act.wait_ge(S["uv"], n - 1)
                nc.scalar.activation(f_sil[:, slot, :], src, ACT.Silu, scale=1.0 / 128).then_inc(S["sil"], 1)

            def sign(n):
                act.wait_ge(S["f_round"], n + 1)
                nc.scalar.activation(f_s[:, :], f_r[:, :], ACT.Sign).then_inc(S["f_sgn"], 1)

            silu(0, 0)
            silu(1, 1)
            for item in AFTER:
                if item[0] == "chan":
                    shared(B, item)
            sign(0)
            silu(2, 0)
            silu(3, 1)
            for item in AFTER[-2:]:
                shared(B, item)
            sign(1)
            act.wait_ge(S["y_out"], NTT)
            sign(2)
            split_wd(0, 0)
            sign(3)
            split_wd(1, 1)
            for n in range(NS, 2 * NS):
                silu(n, n % 2)
                sign(n)
                if n in (5, 6):
                    split_gu(n - 1, (n - 1) % 2, (n - 1) % 2, n)
                    split_wd(n - 3, (n - 3) % 2)
            with act.Fori(NS, NI - 3, 2) as i:
                for u in range(2):
                    for half in range(NHALF):
                        silu(NHALF * (i + u) + half, half)
                        sign(NHALF * (i + u) + half)
                    split_gu(i + u + 2, u, u, NHALF * (i + u + 1))
                    split_wd(i + u, u)
            for i in (NI - 3, NI - 2, NI - 1):
                for half in range(NHALF):
                    silu(NHALF * i + half, half)
                    sign(NHALF * i + half)
                if i == NI - 3:
                    split_gu(NI - 1, 0, 0, NHALF * (NI - 2))
                split_wd(i, i % 2)
            for t in range(NTT):
                r = t % 2
                act.wait_ge(S["dn"], t + 1)
                if t >= 2:
                    act.wait_ge(S["o_clip"], t - 1)
                nc.scalar.activation(d_sb[:, r, :], bD[r][:, :], ACT.Copy, scale=128.0).then_inc(S["d_out"], 1)
                act.wait_ge(S["o_round"], t + 1)
                if t >= 2:
                    act.wait_ge(S["z_var"], t - 1)
                nc.scalar.activation(d_s[:, r, :], d_r[:, r, :], ACT.Sign).then_inc(S["o_sgn"], 1)

        @block.vector
        def _(dve):
            def w_lo(u):
                w, c = divmod(u * 2, NC)
                dve.wait_ge(S["w_hi"], u + 1)
                c = slice(c, c + 2)
                hi, lo = (WQH[:, w, c, :], WQL[:, w, c, :]) if w < 3 else (WOH[:, c, :], WOL[:, c, :])
                nc.vector.tensor_tensor(lo, w_raw[:, w, c, :], hi.bitcast(F32), ALU.subtract).then_inc(S["w_lo"], 1)

            def rotate(n, m, bank):
                a, t = divmod(m, NT)
                dve.wait_ge(S["t1"], n * 4 + m + 1)
                wait(dve, "lo", n * 8 - 3 + m)
                cos = K[:, K_ROT + 4 * t + 2 * a:K_ROT + 4 * t + 2 * a + 1]
                src = shared_bank[bank][:, :].rearrange("p (h e d) -> p h e d", e=2, d=D // 2)
                sn = T1[:, :].rearrange("p (h e d) -> p h e d", e=2, d=D // 2)
                dst = RQ[:, m, :].rearrange("p (h e d) -> p h e d", e=2, d=D // 2)
                nc.vector.scalar_tensor_tensor(out=dst[:, :, 0, :], in0=src[:, :, 0, :], scalar=cos, in1=sn[:, :, 1, :],
                                               op0=ALU.mult, op1=ALU.subtract)
                nc.vector.scalar_tensor_tensor(out=dst[:, :, 1, :], in0=src[:, :, 1, :], scalar=cos, in1=sn[:, :, 0, :],
                                               op0=ALU.mult, op1=ALU.add).then_inc(S["rope"], 1)

            def scores(b, h):
                dve.wait_ge(S["sc"], b * H + h + 1)
                wait(dve, "pr", b * H + h - R_SM + 1)
                if not isinstance(b, int):
                    dve.sem_inc(S["dve_tick"], 1)
                for t in range(NT):
                    cols = slice(0, P) if t == 0 else slice(P, SW)
                    m = mask[:, P:2 * P] if t == 0 else mask
                    last = nc.vector.tensor_tensor_reduce(out=SM[:, h % R_SM, cols], in0=bS[h % R_S][:, cols], in1=m, scale=1.0,
                                                          scalar=HUGE, op0=ALU.add, op1=ALU.min, accum_out=nb[:, h, t:t + 1])
                last.then_inc(S["sm"], 1)

            def probs(b, h):
                dve.wait_ge(S["pt"], b * H + h + 1)
                wait(dve, "pv", b * NG + (h - R_PTS) // 4 + 1)
                nc.vector.tensor_copy(PTS[:, h % R_PTS, :], bPT[h % R_PT][:, 0:SW]).then_inc(S["pts"], 1)

            def normalise(n, u, bank):
                half, t = divmod(u, NT)
                dve.wait_ge(S["ob"], n * 4 + u + 1)
                src = shared_bank[bank][:, :].rearrange("p (h d) -> p h d", d=32)
                r = rden[:, u, :].rearrange("p (h o) -> p h o", o=1)
                nc.vector.reciprocal(r, src[:, :, D:D + 1]).then_inc(S["rd"], 1)
                wait(dve, "oT", n * 2)
                dve.wait_ge(S["rd"], n * 4 + u + 1)
                nc.vector.tensor_tensor(ON[:, t, half * (C // 2):(half + 1) * (C // 2)].rearrange("p (h d) -> p h d", d=D),
                                        src[:, :, 0:D], r.broadcast_to((P, H // 2, D)), ALU.mult).then_inc(S["on"], 1)

            def chan_lo(n, k, bank):
                dve.wait_ge(S["oh"], n * 2 + k + 1)
                nc.vector.tensor_tensor(OL[:, 2 * k:2 * k + 2, :], shared_bank[bank][:, :].rearrange("p (c t) -> p c t", c=2),
                                        OH[:, 2 * k:2 * k + 2, :].bitcast(F32), ALU.subtract).then_inc(S["ol"], 1)

            def residual(n, t, bank):
                dve.wait_ge(S["xn_in"], n * 16 + 16)
                dve.wait_ge(S["yp"], n * NT + t + 1)
                nc.vector.tensor_tensor(RES[:, t, :], shared_bank[bank][:, :], RES[:, t, :], ALU.add).then_inc(S["res"], 1)
                dve.wait_ge(S["res"], (n + 1) * NT + t + 1)
                nc.vector.bn_stats(st[:, t, :], RES[:, t, :]).then_inc(S["ln_dve"], 1)
                dve.wait_ge(S["ln_dve"], n * 2 * NT + 2 * t + 1)
                if not isinstance(n, int):
                    dve.sem_inc(S["dve_tick"], 1)
                nc.vector.bn_aggr(mv[:, t, 0:2], st[:, t, :]).then_inc(S["ln_dve"], 1)
                dve.wait_ge(S["ln_dve"], n * 2 * NT + 2 * t + 2)
                nc.vector.tensor_scalar(mv[:, t, 2:3], mv[:, t, 1:2], EPS, None, ALU.add).then_inc(S["ln_var"], 1)

            def layernorm(n, t):
                dve.wait_ge(S["ln_rstd"], n * NT + t + 1)
                nc.vector.tensor_scalar(Y[:, bass.ds(n * (NT * C) + t * C, C)], RES[:, t, :], mv[:, t, 0:1], mv[:, t, 3:4],
                                        ALU.subtract, ALU.mult).then_inc(S["y_out"], 1)

            def y_lo(t, bank):
                half, r = divmod(t, NTT // NHALF)
                dve.wait_ge(S["yh"], t + 1)
                nc.vector.tensor_tensor(YL[half][:, :, r * P:(r + 1) * P], shared_bank[bank][:, :].rearrange("p (c t) -> p c t", c=NC),
                                        YH[half][:, :, r * P:(r + 1) * P].bitcast(F32), ALU.subtract).then_inc(S["yl"], 1)

            def shared(b, item):
                kind, n, rel, bank, _, _ = item
                if kind == "proj" and n < 4:
                    rotate(b + rel, n, bank)
                elif kind == "back":
                    normalise(b + rel, n, bank)
                elif kind == "chan":
                    chan_lo(b + rel, n, bank)
                elif kind == "outp":
                    residual(b + rel, n, bank)
                elif kind == "yt":
                    y_lo(n, bank)

            def run(b, kind):
                if kind == "before":
                    nc.vector.memset(QS[:, :, :, :].rearrange("p a t (h k) -> p (a t h) k", k=SLOT)[:, :, KROWS:SLOT].bitcast(F32), 0.0).then_inc(S["pads"], 1)
                    dve.sem_inc(S["res"], NT)
                    dve.wait_ge(S["xh"], 1)
                    nc.vector.tensor_tensor(XL[:, :, :], XR[:, :, :], XH[:, :, :].bitcast(F32), ALU.subtract).then_inc(S["xl"], 1)
                    for u in range(4):
                        w_lo(u)
                    dve.wait_ge(S["k_in"], 16)
                    for m in range(4):
                        rotate(0, m, m)
                    w_lo(6)
                    w_lo(7)
                    dve.wait_ge(S["v_lo"], 2)
                    return
                for s in steps(kind):
                    if kind != "after":
                        scores(b, s)
                    for n, h in trailing(b, kind, s, LAG_PT):
                        probs(n, h)
                    if kind == "after":
                        for item in AFTER[:2]:
                            if s == item[4] + 2:
                                shared(b, item)
                        continue
                    for item in finished_dve(kind, s):
                        shared(b, item)
                    if kind != "first":
                        for item in finished_dve(kind, s - 1):
                            if item[0] == "outp":
                                layernorm(b - 1, item[1])
                if kind == "middle":
                    layernorm(b - 1, 1)

            rounds(dve, run)

            def silu_up(n, slot, v):
                early = isinstance(n, int) and n < 2
                dve.wait_ge(S["sil"], n + 1)
                dve.wait_ge(S["gu_out" if early else "u_mm"], 2 * n + 2 if early else n + 1)
                nc.vector.tensor_tensor(f_v[:, v, :], f_sil[:, slot, :], f_v[:, v, :] if early else bU[slot][:, :], ALU.mult).then_inc(S["uv"], 1)

            def truncate(n, at, v):
                k = [n * 4]

                def link(ins):
                    ins.then_inc(S["f_dve"], 1)
                    k[0] = k[0] + 1
                    dve.wait_ge(S["f_dve"], k[0])

                dve.wait_ge(S["uv"], n + 1)
                link(nc.vector.tensor_scalar(f_c[:, :], f_v[:, v, :], -128.0, 127.0, ALU.max, ALU.min))
                nc.vector.tensor_scalar(f_r[:, :], f_c[:, :], MAGIC, -MAGIC, ALU.add, ALU.add).then_inc(S["f_round"], 1)
                dve.wait_ge(S["f_round"], n + 1)
                link(nc.vector.tensor_tensor(f_d[:, 0, :], f_r[:, :], f_c[:, :], ALU.subtract))
                link(nc.vector.tensor_tensor(f_e[:, :], f_d[:, 0, :], f_r[:, :], ALU.mult))
                dve.wait_ge(S["f_sgn"], n + 1)
                link(nc.vector.scalar_tensor_tensor(out=f_d[:, 1, :], in0=f_e[:, :], scalar=0.0, in1=f_s[:, :], op0=ALU.is_gt, op1=ALU.mult))
                nc.vector.tensor_tensor(IQ[:, bass.ds(at, HALF)], f_r[:, :], f_d[:, 1, :], ALU.subtract).then_inc(S["iq"], 1)

            for item in AFTER[2:]:
                if item[0:2] == ("outp", 0):
                    silu_up(0, 0, 0)
                    silu_up(1, 1, 1)
                    truncate(0, 0, 0)
                    silu_up(2, 0, 2)
                if item[0:2] == ("yt", 6):
                    for t in range(NT):
                        layernorm(B - 1, t)
                shared(B, item)
            truncate(1, B * T, 1)
            silu_up(3, 1, 3)
            truncate(2, 2 * B * T, 2)
            truncate(3, 3 * B * T, 3)
            for n in range(NS, 2 * NS):
                silu_up(n, n % 2, n % 4)
                truncate(n, (n - NS) * B * T + HALF, n % 4)
            with dve.Fori(NS, NI - 1, 2) as i:
                for u in range(2):
                    for half in range(NHALF):
                        silu_up(NHALF * (i + u) + half, half, 2 * u + half)
                        truncate(NHALF * (i + u) + half, (i + u) * (B * T) + half * HALF, 2 * u + half)
            for half in range(NHALF):
                silu_up(NHALF * (NI - 1) + half, half, half)
                truncate(NHALF * (NI - 1) + half, (NI - 1) * (B * T) + half * HALF, half)

            def clip(t):
                dve.wait_ge(S["d_out"], t + 1)
                nc.vector.tensor_scalar(d_c[:, t % 2, :], d_sb[:, t % 2, :], -128.0, 127.0, ALU.max, ALU.min).then_inc(S["o_clip"], 1)

            def round_(t):
                dve.wait_ge(S["o_clip"], t + 1)
                nc.vector.tensor_scalar(d_r[:, t % 2, :], d_c[:, t % 2, :], MAGIC, -MAGIC, ALU.add, ALU.add).then_inc(S["o_round"], 1)

            def second_layernorm(t):
                r = t % 2
                dve.wait_ge(S["z_rstd"], t + 1)
                if t >= 2:
                    dve.wait_ge(S[f"stored{r}"], 16 * (t // 2))
                nc.vector.tensor_scalar(o[:, r, :], z[:, r, :], mz[:, r, 0:1], mz[:, r, 3:4], ALU.subtract, ALU.mult).then_inc(S["z_out"], 1)

            clip(0)
            round_(0)
            for t in range(NTT):
                r = t % 2
                if t + 1 < NTT:
                    clip(t + 1)
                dve.wait_ge(S["o_sgn"], t + 1)
                dve.wait_ge(S["o_pool"], 2 * t + 2)
                nc.vector.scalar_tensor_tensor(out=d_d[:, r, :], in0=d_e[:, r, :], scalar=0.0, in1=d_s[:, r, :],
                                               op0=ALU.is_gt, op1=ALU.mult).then_inc(S["o_dve"], 1)
                if t + 1 < NTT:
                    round_(t + 1)
                dve.wait_ge(S["o_dve"], t * 5 + 1)
                nc.vector.tensor_tensor(z[:, r, :], d_r[:, r, :], d_d[:, r, :], ALU.subtract).then_inc(S["o_dve"], 1)
                if t >= 1:
                    second_layernorm(t - 1)
                dve.wait_ge(S["o_dve"], t * 5 + 2)
                nc.vector.tensor_tensor(z[:, r, :], z[:, r, :], Y[:, t * C:(t + 1) * C], ALU.add).then_inc(S["o_dve"], 1)
                dve.wait_ge(S["o_dve"], t * 5 + 3)
                nc.vector.bn_stats(sz[:, r, :], z[:, r, :]).then_inc(S["o_dve"], 1)
                dve.wait_ge(S["o_dve"], t * 5 + 4)
                nc.vector.bn_aggr(mz[:, r, 0:2], sz[:, r, :]).then_inc(S["o_dve"], 1)
                dve.wait_ge(S["o_dve"], t * 5 + 5)
                nc.vector.tensor_scalar(mz[:, r, 2:3], mz[:, r, 1:2], EPS, None, ALU.add).then_inc(S["z_var"], 1)
            second_layernorm(NTT - 1)

        @block.tensor
        def _(pe):
            def product(dst, c, ah, al, bh, bl):
                nc.tensor.matmul(dst, ah, bh, start=(c == 0), stop=False)
                nc.tensor.matmul(dst, ah, bl, start=False, stop=False)
                return nc.tensor.matmul(dst, al, bh, start=False, stop=(c == NC - 1))

            def wait_read(b, kind, item):
                mine = [i for i in SHARED[kind] if i[3] == item[3]]
                at = mine.index(item)
                if at:
                    name, n, rel = mine[at - 1][:3]
                elif kind == "before":
                    return
                else:
                    name, n, rel = [i for i in SHARED[BEFORE[kind]] if i[3] == item[3]][-1][:3]
                    rel -= 1
                sem, per, count = {"back": ("on", 4, n + 1), "chan": ("ol", 2, n + 1), "outp": ("res", NT, NT + n + 1), "yt": ("yl", 0, n + 1), "gate": ("gu_out", 0, 2 * n + 1), "up": ("gu_out", 0, 2 * n + 2),
                                   "proj": ("rope", 4, n + 1) if n < 4 else ("v_sb", 2, n - 3)}[name]
                wait(pe, sem, (b + rel) * per + count)

            def weights_by_y(dst, slot, k, c, half):
                wh, wl = (m[:, slot, :].rearrange("p (k c n) -> p k c n", k=2, c=NC) for m in (GH, GL))
                return product(dst[:, :], c, wh[:, k, c, :], wl[:, k, c, :], YH[half][:, c, :], YL[half][:, c, :])

            def shared(b, kind, item, c):
                what, n, rel, bank, _, _ = item
                m = b + rel
                dst = shared_bank[bank]
                if c == 0:
                    wait_read(b, kind, item)
                if what == "proj":
                    w, t = divmod(n, NT)
                    if c == 0:
                        pe.wait_ge(S["xh"], m + 1)
                        pe.wait_ge(S["xl"], m + 1)
                    if c % 2 == 0:
                        pe.wait_ge(S["w_lo" if w < 2 else "v_lo"], (2 * w if w < 2 else 0) + c // 2 + 1)
                    tok = slice(t * P, (t + 1) * P)
                    last = product(dst[:, :], c, XH[:, c, tok], XL[:, c, tok], WQH[:, w, c, :], WQL[:, w, c, :])
                    done = "proj"
                elif what == "back":
                    half, t = divmod(n, NT)
                    pe.wait_ge(S["ot"], m * NG + (half + 1) * (NG // 2))
                    for g in range(NG // 2):
                        last = nc.tensor.transpose(dst[:, g * P:(g + 1) * P], OT[:, half * (NG // 2) + g, t * P:(t + 1) * P], ident)
                    done = "ob"
                elif what == "chan":
                    pe.wait_ge(S["on"], m * 4 + 2 * (n + 1))
                    for i in range(2):
                        for t in range(NT):
                            last = nc.tensor.transpose(dst[:, i * T + t * P:i * T + (t + 1) * P],
                                                       ON[:, t, (2 * n + i) * P:(2 * n + i + 1) * P], ident)
                    done = "oT"
                elif what == "outp":
                    if c == 0:
                        pe.wait_ge(S["w_lo"], 6)
                        pe.wait_ge(S["ol"], m * 2 + 2)
                    tok = slice(n * P, (n + 1) * P)
                    last = product(dst[:, :], c, OH[:, c, tok], OL[:, c, tok], WOH[:, c, :], WOL[:, c, :])
                    done = "yp"
                elif what in ("gate", "up"):
                    if c == 0:
                        pe.wait_ge(S["gu_lo"], n + 1)
                        pe.wait_ge(S["yl"], NTT // 2)
                    last = weights_by_y(dst, n, what == "up", c, 0)
                    done = "g_mm" if what == "gate" else "u_mm"
                else:
                    pe.wait_ge(S["y_out"], n + 1)
                    for i in range(NC):
                        last = nc.tensor.transpose(dst[:, i * P:(i + 1) * P], Y[:, n * C + i * P:n * C + (i + 1) * P], ident)
                    done = "yt"
                if c == chunks(item) - 1:
                    last.then_inc(S[done], 1)

            def stack_t(b, j):
                if j % (NBLK // 2) == 0:
                    pe.wait_ge(S["lo"], b * 8 + (4 if j == 0 else 8))
                wait(pe, "qkt", b * NBLK + j)
                for a in range(2):
                    for t in range(NT):
                        last = nc.tensor.transpose(bTR[:, a * T + t * P:a * T + (t + 1) * P].bitcast(F32R),
                                                   QS[:, a, t, j * P:(j + 1) * P], identr[:, :])
                last.then_inc(S["tr"], 1)

            def scores(b, h):
                j, half = divmod(h, 2)
                rows = slice(half * SLOT, half * SLOT + KROWS)
                pe.wait_ge(S["qkt"], b * NBLK + j + 1)
                wait(pe, "sm", b * H + h - R_S + 1)
                q = QKT[rows, j % R_QKT, 0, :]
                k = QKT[rows, j % R_QKT, 1, :]
                nc.tensor.matmul(bS[h % R_S][:, 0:P], q[:, 0:P], k[:, 0:P], start=True, stop=True)
                nc.tensor.matmul(bS[h % R_S][:, P:SW], q[:, P:T], k[:, 0:T], start=True, stop=True).then_inc(S["sc"], 1)

            def probs_t(b, h):
                pe.wait_ge(S["pr"], b * H + h + 1)
                wait(pe, "pts", b * H + h - R_PT + 1)
                for i in range(3):
                    last = nc.tensor.transpose(bPT[h % R_PT][:, i * P:(i + 1) * P], PR[:, h % R_P, i * P:(i + 1) * P], ident)
                last.then_inc(S["pt"], 1)

            def pv(b, g):
                wait(pe, "ot", b * NG + g)
                pe.wait_ge(S["pts"], b * H + 4 * (g + 1))
                if g == 0:
                    pe.wait_ge(S["v_sb"], b * 2 + 2)
                for key, to, cols in ((0, slice(0, T), slice(0, T)), (1, slice(P, T), slice(T, SW))):
                    for r in range(4):
                        h = 4 * g + r
                        last = nc.tensor.matmul(bAV[32 * r:32 * r + 32, to], V[:, key, h, :], PTS[:, h % R_PTS, cols],
                                                start=(key == 0), stop=(key == 1))
                last.then_inc(S["pv"], 1)

            def gate(n, i, slot, half, bank):
                pe.wait_ge(S["gu_lo"], i + 1)
                if not (isinstance(n, int) and n < 4):
                    pe.wait_ge(S["sil"], n - 1)
                for c in range(NC):
                    last = weights_by_y(bG[bank], slot, 0, c, half)
                last.then_inc(S["g_mm"], 1)

            def up(n, slot, half, bank):
                if not (isinstance(n, int) and n < 4):
                    pe.wait_ge(S["uv"], n - 1)
                for c in range(NC):
                    last = weights_by_y(bU[bank], slot, 1, c, half)
                last.then_inc(S["u_mm"], 1)

            def run(b, kind):
                if kind == "before":
                    for item in SHARED[kind]:
                        for c in range(NC):
                            shared(b, kind, item, c)
                    pe.wait_ge(S["pads"], 1)
                    pe.wait_ge(S["identr"], 1)
                    for item in VALUES:
                        for c in range(NC):
                            shared(0, "first", item, c)
                            if item == VALUES[1] and c % 2:
                                stack_t(0, c // 2)
                for s in steps(kind):
                    for n, j in leading(b, kind, s):
                        stack_t(n, j)
                    if kind != "after":
                        scores(b, s)
                    for n, h in trailing(b, kind, s, LAG_PT):
                        probs_t(n, h)
                    for n, h in trailing(b, kind, s, LAG_AV):
                        if h % 4 == 3:
                            pv(n, h // 4)
                    for item in AFTER[:2] if kind == "after" else [] if kind == "before" else SHARED[kind]:
                        k, n = s - item[4], item[5]
                        if 0 <= k < n and not (kind == "first" and item in VALUES):
                            for c in range(chunks(item) * k // n, chunks(item) * (k + 1) // n):
                                shared(b, kind, item, c)
                if kind == "after":
                    for item in AFTER[2:]:
                        if item[0:2] == ("chan", 0):
                            pe.wait_ge(S["sm"], B * H)
                            gate(2, 2, 2, 0, 0)
                        if item[0:2] == ("outp", 0):
                            pe.wait_ge(S["pts"], B * H)
                            up(2, 2, 0, 0)
                        if item[0:2] == ("yt", 6):
                            gate(3, 3, 3, 0, 1)
                            up(3, 3, 0, 1)
                        for c in range(chunks(item)):
                            shared(b, kind, item, c)

            pe.wait_ge(S["v_init"], 2)
            for _ in range(3):
                nc.tensor.matmul(bPT[0][:, :], V[:, 0, 0:4, :], V[:, 0, 0:16, :], start=True, stop=True)
            pe.wait_ge(S["k_in"], 16)
            rounds(pe, run)

            pe.wait_ge(S["yl"], NTT)
            for n in range(NS, 2 * NS):
                gate(n, n - NS, n - NS, 1, n % 2)
                up(n, n - NS, 1, n % 2)
            with pe.Fori(NS, NI - 1, 2) as i:
                for u in range(2):
                    for half in range(NHALF):
                        gate(NHALF * (i + u) + half, i + u, u, half, half)
                        up(NHALF * (i + u) + half, u, half, half)
            for half in range(NHALF):
                gate(NHALF * (NI - 1) + half, NI - 1, 0, half, half)
                up(NHALF * (NI - 1) + half, 0, half, half)
            for t in range(NTT):
                wait(pe, "d_out", t - 1)
                for i in range(NI):
                    if t == 0 and i == 0:
                        pe.wait_ge(S["wd_lo"], NI - 3)
                        pe.wait_ge(S["iq"], NHALF * (NI - 3))
                    if t == 0 and i >= NI - 3:
                        pe.wait_ge(S["wd_lo"], i + 1)
                        pe.wait_ge(S["iq"], NHALF * i + 1)
                    if t == NTT // NHALF and i == NI - 1:
                        pe.wait_ge(S["iq"], NHALF * NI)
                    a = IQ[:, i * B * T + t * P:i * B * T + (t + 1) * P]
                    nc.tensor.matmul(bD[t % 2][:, :], a, DH[:, i, :], start=(i == 0), stop=False)
                    last = nc.tensor.matmul(bD[t % 2][:, :], a, DL[:, i, :], start=False, stop=(i == NI - 1))
                last.then_inc(S["dn"], 1)


def kernel(**inputs):
    import numpy as np
    import concourse.bacc as bacc
    from concourse.bass_utils import run_bass_kernel_spmd

    def pairs_apart(w):
        return w.reshape(H, D // 2, 2, C).transpose(0, 2, 1, 3).reshape(C, C)

    def padded(w):
        return np.concatenate([w, np.zeros((NI * P - INTER, C), w.dtype)])

    a = {k: np.asarray(v) for k, v in inputs.items()}
    xs = a["L0_attn_x"]
    wqkvo = np.stack([pairs_apart(a["L0_attn_wq"]).T, pairs_apart(a["L0_attn_wk"]).T, a["L0_attn_wv"].T, a["L0_attn_wo"].T])
    gu = np.stack([padded(a["L0_ffn_w_gate"]), padded(a["L0_ffn_w_up"])])
    gu = gu.reshape(2, NI, P, NC, P).transpose(1, 4, 0, 3, 2).reshape(NI, P, 2 * NC * P)
    wd = padded(a["L0_ffn_w_down"].T).reshape(NI, P, C)

    k = np.zeros((P, NK), np.float32)
    k[:, K_ID:K_ID + P] = np.eye(P)
    k[:, K_MASK + P:K_MASK + 2 * P] = np.triu(np.full((P, P), BIG), 1)
    theta = np.arange(T, dtype=np.float32).reshape(NT, P)
    for t in range(NT):
        for j, v in enumerate((-D ** -0.5 * np.cos(theta[t]), -D ** -0.5 * np.sin(theta[t]), np.cos(theta[t]), np.sin(theta[t]))):
            k[:, K_ROT + 4 * t + j] = v
    k[:, K_HALF] = -0.5

    nc = bacc.Bacc("TRN2", target_bir_lowering=False, num_devices=1)
    arrays, args = {}, []
    for name, v in (("xT", xs.transpose(0, 2, 1)), ("x", xs), ("wqkvo", wqkvo), ("wgu", gu), ("wd", wd), ("consts", k)):
        v = np.ascontiguousarray(v)
        arrays[name] = v
        args.append(nc.dram_tensor(name, v.shape, mybir.dt.from_np(v.dtype), kind="ExternalInput").ap())
    args.append(nc.dram_tensor("out", (B * T, C), F32, kind="ExternalOutput").ap())
    layer(nc, *args)
    r = run_bass_kernel_spmd(nc, [arrays], core_ids=[0])
    return r.results[0]["out"].reshape(B, T, C)
```
